# Optimizing a Trainium2 kernel written in Bass

```python
import numpy as np
import jax
import jax.numpy as jnp

def _softmax(x, axis=-1):
    return jax.nn.softmax(x, axis=axis)

def _gelu(x):
    return jax.nn.gelu(x, approximate=True)

def _silu(x):
    return jax.nn.silu(x)

def _sigmoid(x):
    return jax.nn.sigmoid(x)

def _layernorm(x, axis=-1, eps=1e-05):
    m = jnp.mean(x, axis=axis, keepdims=True)
    v = jnp.var(x, axis=axis, keepdims=True)
    return (x - m) / jnp.sqrt(v + eps)

def _scatter_add(tgt, idx, src, axis=0):
    return tgt.at[idx].add(src)

def _segment_sum(src, seg, n):
    return jax.ops.segment_sum(src, seg, n)
kernel_name = 'mk_seq_postln_d1_jaxref_r8_bd0da1'

def setup_inputs(seed: int=0):
    np.random.seed(seed)
    _w = jnp.asarray

    def _L0_attn_setup():
        import jax, jax.numpy as jnp
        import numpy as np
        B, T, D, H = (4, 256, 128, 16)
        HD = D // H
        EPS = 1e-05
        NEG = 10000000000.0
        key = jax.random.key(seed)
        k1, k2, k3 = jax.random.split(key, 3)
        return {'target': jax.random.normal(k1, (B, T, D), dtype=jnp.float32), 'w_qkv': jax.random.normal(k2, (D, 3 * D), dtype=jnp.float32) * 0.02, 'w_proj': jax.random.normal(k3, (D, D), dtype=jnp.float32) * (0.02 / np.sqrt(24.0)), 'b_proj': jnp.zeros((D,), dtype=jnp.float32), 'ln_gamma': jnp.ones((D,), dtype=jnp.float32), 'ln_beta': jnp.zeros((D,), dtype=jnp.float32)}
    _L0_attn_in = _L0_attn_setup()

    def _L0_ffn_setup():
        import jax, jax.numpy as jnp
        import numpy as np
        B, S, D, E, F = (2, 128, 128, 14, 256)
        key = jax.random.key(seed)
        k0, k1, k2, k3 = jax.random.split(key, 4)
        h = jax.random.normal(k0, (B, S, D), jnp.float32)
        gate_w = jax.random.normal(k1, (E, D), jnp.float32) * 0.02
        w1 = jax.random.normal(k2, (E, D, F), jnp.float32) * (1.0 / np.sqrt(D).astype(np.float32))
        b1 = jnp.zeros((E, F), jnp.float32)
        w2 = jax.random.normal(k3, (E, F, D), jnp.float32) * (1.0 / np.sqrt(F).astype(np.float32))
        b2 = jnp.zeros((E, D), jnp.float32)
        return {'h': h, 'gate_w': gate_w, 'w1': w1, 'b1': b1, 'w2': w2, 'b2': b2}
    _L0_ffn_in = _L0_ffn_setup()
    _d = {'L0_attn_target': _L0_attn_in['target'], 'L0_attn_w_qkv': _L0_attn_in['w_qkv'], 'L0_attn_w_proj': _L0_attn_in['w_proj'], 'L0_attn_b_proj': _L0_attn_in['b_proj'], 'L0_attn_ln_gamma': _L0_attn_in['ln_gamma'], 'L0_attn_ln_beta': _L0_attn_in['ln_beta'], 'L0_ffn_gate_w': _L0_ffn_in['gate_w'], 'L0_ffn_w1': _L0_ffn_in['w1'], 'L0_ffn_b1': _L0_ffn_in['b1'], 'L0_ffn_w2': _L0_ffn_in['w2'], 'L0_ffn_b2': _L0_ffn_in['b2']}
    _x0 = _d['L0_attn_target']
    _d['L0_attn_target'] = jax.random.normal(jax.random.fold_in(jax.random.key(seed), 1), (16, 256, 128), dtype=_x0.dtype)
    del _x0
    return _d

def reference(L0_attn_target, L0_attn_w_qkv, L0_attn_w_proj, L0_attn_b_proj, L0_attn_ln_gamma, L0_attn_ln_beta, L0_ffn_gate_w, L0_ffn_w1, L0_ffn_b1, L0_ffn_w2, L0_ffn_b2):

    def _L0_attn_ref(target, w_qkv, w_proj, b_proj, ln_gamma, ln_beta):
        import jax, jax.numpy as jnp
        import numpy as np
        B, T, D, H = (4, 256, 128, 16)
        HD = D // H
        EPS = 1e-05
        NEG = 10000000000.0
        b, t, d = target.shape
        resid = target
        qkv = target @ w_qkv
        q, k, v = jnp.split(qkv, 3, axis=-1)
        q = q.reshape(b, t, H, HD).transpose(0, 2, 1, 3)
        k = k.reshape(b, t, H, HD).transpose(0, 2, 1, 3)
        v = v.reshape(b, t, H, HD).transpose(0, 2, 1, 3)
        scores = jnp.einsum('bhqd,bhkd->bhqk', q, k) * (1.0 / np.sqrt(HD))
        causal = (jnp.arange(t)[:, None] >= jnp.arange(t)[None, :]).astype(scores.dtype)
        scores = scores * causal - (1.0 - causal) * NEG
        attn = jax.nn.softmax(scores, axis=-1)
        out = jnp.einsum('bhqk,bhkd->bhqd', attn, v)
        out = out.transpose(0, 2, 1, 3).reshape(b, t, d)
        proj = out @ w_proj + b_proj
        x = proj + resid
        mu = jnp.mean(x, axis=-1, keepdims=True)
        var = jnp.var(x, axis=-1, keepdims=True)
        return (x - mu) * jax.lax.rsqrt(var + EPS) * ln_gamma + ln_beta

    def _L0_ffn_ref(h, gate_w, w1, b1, w2, b2):
        import jax, jax.numpy as jnp
        import numpy as np
        B, S, D, E, F = (2, 128, 128, 14, 256)
        Bb, Ss, Dd = h.shape
        x = h.reshape(Bb * Ss, Dd)
        logits = x @ gate_w.T
        probs = jax.nn.softmax(logits, axis=-1)
        top2_p, top2_i = jax.lax.top_k(probs, 2)
        w = top2_p / jnp.maximum(top2_p.sum(-1, keepdims=True), 1e-10)
        hh = jnp.einsum('nd,edf->nef', x, w1) + b1
        hh = jax.nn.gelu(hh, approximate=False)
        all_out = jnp.einsum('nef,efd->ned', hh, w2) + b2
        n = jnp.arange(x.shape[0])
        out0 = all_out[n, top2_i[:, 0]]
        out1 = all_out[n, top2_i[:, 1]]
        moe_out = w[:, 0:1] * out0 + w[:, 1:2] * out1
        result = jnp.clip(x + moe_out, -100.0, 100.0).reshape(Bb, Ss, Dd)
        return result
    x = L0_attn_target
    x = _layernorm(x + _L0_attn_ref(x, L0_attn_w_qkv, L0_attn_w_proj, L0_attn_b_proj, L0_attn_ln_gamma, L0_attn_ln_beta), axis=-1)
    x = _layernorm(x + _L0_ffn_ref(x, L0_ffn_gate_w, L0_ffn_w1, L0_ffn_b1, L0_ffn_w2, L0_ffn_b2), axis=-1)
    return x

_drawn_inputs = setup_inputs


def setup_inputs(seed=0):
    import zlib

    import numpy as np

    out = dict(_drawn_inputs(seed))
    spreads = {'L0_attn_b_proj': (0.0, 0.1),
     'L0_attn_ln_gamma': (1.0, 0.2),
     'L0_attn_ln_beta': (0.0, 0.1),
     'L0_ffn_b1': (0.0, 0.349),
     'L0_ffn_b2': (0.0, 0.1)}
    factors = {'L0_attn_w_qkv': 8.0, 'L0_attn_w_proj': 8.0}
    for name, (base, spread) in spreads.items():
        noise = np.random.default_rng([zlib.crc32(name.encode()), seed]).standard_normal(out[name].shape)
        drawn = base * np.exp(spread * noise) if base else spread * noise
        out[name] = jnp.asarray(drawn.astype(out[name].dtype))
    for name, factor in factors.items():
        out[name] = (out[name] * factor).astype(out[name].dtype)
    return out
```

```python
from contextlib import ExitStack

import concourse.bass as bass
from concourse import mybir

F32 = mybir.dt.float32
BF16 = mybir.dt.bfloat16
U32 = mybir.dt.uint32
ALU = mybir.AluOpType
ACT = mybir.ActivationFunctionType
X = mybir.AxisListType.X

P = 128
H = 16
EPS = 1e-5
NEG = -1e30


def after(eng, sem, count):
    if not isinstance(count, int) or count > 0:
        eng.wait_ge(sem, count)


def transformer_layer(nc, x, w_qkv, w_proj, b_proj, ln_gamma, ln_beta, gate_w, w1, b1, w2, b2, out):
    B, T, D = x.shape
    E, _, F = w1.shape
    HD = D // H
    SCALE = float(HD) ** -0.5
    TT = T // P
    NT = B * TT
    FC = F // P
    NP = H // 2
    KQ = 6 * HD
    assert D == P and T == 2 * P and H * HD == P

    def on(s):
        return not isinstance(s, int) or 0 <= s < B

    x_tiles = x.rearrange("b (i p) d -> b p i d", p=P)
    out_chunks = out.rearrange("(c b) (i p) d -> c p (b i) d", b=2, p=P)

    with ExitStack() as ctx:
        def sb(name, shape, dt=F32):
            return ctx.enter_context(nc.sbuf_tensor(name, shape, dt))

        def ps(name, shape, dt=F32):
            return ctx.enter_context(nc.psum_tensor(name, shape, dt))

        def sem(name):
            return ctx.enter_context(nc.semaphore(name))

        ident = sb("ident", [P, P])
        ident_bf = sb("ident_bf", [P, P], BF16)
        causal_neg = sb("causal_neg", [P, P], BF16)
        ones_row = sb("ones_row", [1, P])
        minus_half = sb("minus_half", [P, 4])
        expert_no = sb("expert_no", [P, E])
        wqk_raw = sb("wqk_raw", [P, 3 * D])
        wqk = sb("wqk", [P, 2, D])
        wproj = sb("wproj", [P, D])
        gate_raw = sb("gate_raw", [E, D])
        gate_t = sb("gate_t", [P, E])
        bproj_all = sb("bproj_all", [P, D])
        gamma_all = sb("gamma_all", [P, D])
        beta_all = sb("beta_all", [P, D])
        w1_sb = sb("w1_sb", [P, E, F])
        w2_sb = sb("w2_sb", [P, E, FC, D])
        b1_sb = sb("b1_sb", [P, E * FC])
        b2_sb = sb("b2_sb", [1, E * D])
        xin = sb("xin", [P, 3, TT, D])
        xres = sb("xres", [P, 3, TT, D])
        xT = sb("xT", [P, 3, T])
        part_h = sb("part_h", [P, 2, T], BF16)
        part_m = sb("part_m", [P, 2, T], BF16)
        part_l = sb("part_l", [P, 2, T], BF16)
        rest = sb("rest", [P, 2, T])
        v_aug = sb("v_aug", [P, 3, TT, H, 32])
        q_stack = sb("q_stack", [P, 3, H, T], BF16)
        k_stack = sb("k_stack", [P, 3, H, T], BF16)
        row_max = sb("row_max", [P, 3, H, TT])
        shift = sb("shift", [P, 3, 2, H, TT], BF16)
        shift_t = sb("shift_t", [2 * H * TT, 3, P], BF16)
        probs = sb("probs", [P, NP, 3 * T])
        heads_t = sb("heads_t", [P, 4, T])
        inv_sum = sb("inv_sum", [P, TT, H])
        heads = sb("heads", [P, TT, D])
        heads_n_t = sb("heads_n_t", [P, T])
        x_bproj = sb("x_bproj", [P, TT, D])
        x_beta = sb("x_beta", [P, TT, D])
        y = sb("y", [P, TT, D])
        stats = sb("stats", [P, TT, 6])
        moments = sb("moments", [P, TT, 2])
        var_eps = sb("var_eps", [P, TT])
        rstd = sb("rstd", [P, TT])
        yn = sb("yn", [P, TT, D])
        yg = sb("yg", [P, TT, D])
        ys = sb("ys", [P, TT, D])
        stats2 = sb("stats2", [P, TT, 6])
        moments2 = sb("moments2", [P, TT, 2])
        var_eps2 = sb("var_eps2", [P, TT])
        rstd2 = sb("rstd2", [P, TT])
        x2 = sb("x2", [P, 3, TT, D])
        x2_all = sb("x2_all", [P, B, TT * D])
        x2T = sb("x2T", [P, 3, T])
        x2T_all = sb("x2T_all", [P, B, T])
        logits = sb("logits", [P, 3, TT, E])
        top_v = sb("top_v", [P, TT, 8])
        top_i = sb("top_i", [P, TT, 8], U32)
        top_v_all = sb("top_v_all", [P, B, TT, 2])
        top_i_all = sb("top_i_all", [P, B, TT, 2])

        CH = 2 * TT
        NCH = NT // CH
        diff = sb("diff", [P, NT])
        exp2 = sb("exp2", [P, NT])
        esum = sb("esum", [P, NT])
        wgt = sb("wgt", [P, NT, 2])
        chosen = sb("chosen", [P, NT, E])
        weights = sb("weights", [P, 2, NT, E])
        hT = q_stack[:, 0].rearrange("p h q -> p (h q)").bitcast(F32).rearrange("p (n q) -> p n q", n=4)
        acc = sb("acc", [P, CH, D])
        clipped = sb("clipped", [P, CH, D])
        x3 = sb("x3", [P, CH, D])
        stats3 = sb("stats3", [P, CH, 6])
        moments3 = sb("moments3", [P, CH, 2])
        var_eps3 = sb("var_eps3", [P, CH])
        rstd3 = sb("rstd3", [P, CH])
        fin = sb("fin", [P, CH, D])

        S = [ps(f"S{i}", [P, 1024]) for i in range(2)]
        M = [ps(f"M{i}", [P, 512]) for i in range(2)]
        O = ps("O", [P, 512])
        G = ps("G", [P, 512])
        G_bf = G[:, :].bitcast(BF16)
        HB = [S[i // 2][:, (i % 2) * 512:(i % 2) * 512 + 512] for i in range(4)]

        weights_in = sem("weights_in")
        experts_in = sem("experts_in")
        consts = sem("consts")
        consts_v = sem("consts_v")
        consts_p = sem("consts_p")
        gate_turned = sem("gate_turned")
        x_in = [sem(f"x_in{i}") for i in range(3)]
        xres_in = [sem(f"xres_in{i}") for i in range(3)]
        stacked = sem("stacked")
        shifted = sem("shifted")
        xT_ready = sem("xT_ready")
        xT_copied = sem("xT_copied")
        qk_ready = sem("qk_ready")
        h_split = sem("h_split")
        rest_left = sem("rest_left")
        m_split = sem("m_split")
        l_split = sem("l_split")
        v_ready = sem("v_ready")
        v_copied = sem("v_copied")
        m_ready = sem("m_ready")
        m_reduced = sem("m_reduced")
        shift_hi = sem("shift_hi")
        shift_made = sem("shift_made")
        shift_turned = sem("shift_turned")
        shift_copied = sem("shift_copied")
        s_ready = sem("s_ready")
        exp_done = sem("exp_done")
        masked = sem("masked")
        pv_done = sem("pv_done")
        o_copied = sem("o_copied")
        o_turned = sem("o_turned")
        inverted = sem("inverted")
        o_normed = sem("o_normed")
        on_turned = sem("on_turned")
        on_copied = sem("on_copied")
        proj_ready = sem("proj_ready")
        residuals = sem("residuals")
        y_ready = sem("y_ready")
        stats_done = sem("stats_done")
        var_done = sem("var_done")
        rstd_done = sem("rstd_done")
        yn_done = sem("yn_done")
        yg_done = sem("yg_done")
        ys_done = sem("ys_done")
        stats2_done = sem("stats2_done")
        var2_done = sem("var2_done")
        rstd2_done = sem("rstd2_done")
        x2_done = sem("x2_done")
        x2_kept = sem("x2_kept")
        x2T_ready = sem("x2T_ready")
        x2T_copied = sem("x2T_copied")
        x2T_kept = sem("x2T_kept")
        gate_ready = sem("gate_ready")
        logits_done = sem("logits_done")
        top_done = sem("top_done")
        index_done = sem("index_done")
        top_kept = sem("top_kept")
        ones_made = sem("ones_made")
        numbered = sem("numbered")
        diff_done = sem("diff_done")
        exp2_done = sem("exp2_done")
        wt = sem("wt")
        h_ready = sem("h_ready")
        gelu_done = sem("gelu_done")
        ye_ready = sem("ye_ready")
        y_used = sem("y_used")
        moe = sem("moe")
        moe_aggr = sem("moe_aggr")
        moe_var = sem("moe_var")
        moe_rstd = sem("moe_rstd")
        fin_done = sem("fin_done")
        out_sent = sem("out_sent")

        FIRST, LAST = 5, 5 + (B - 5) // 3 * 3

        def run(eng, body):
            for t in range(FIRST):
                body(t, t % 3, t // 3)
            with eng.Fori(0, (LAST - FIRST) // 3) as i:
                for k in range(3):
                    body(i * 3 + (FIRST + k), (FIRST + k) % 3, i + (FIRST + k) // 3)
            for t in range(LAST, B + 4):
                body(t, t % 3, t // 3)

        M_UNITS = []
        for p in range(NP):
            M_UNITS.append((1, 2 * p, 2))
            if p % 2:
                M_UNITS.append((0, 2 * p - 2, 4))
        NM = len(M_UNITS)

        def s_unit(t, u):
            return (t - 2, u - 2) if u >= 2 else (t - 3, u + NP - 2)

        def pv_quad(t, u):
            return {1: (t - 3, 2), 3: (t - 3, 3), 5: (t - 2, 0), 7: (t - 2, 1)}.get(u)

        def wait_apart(eng, sem, count):
            if not isinstance(count, int):
                count = eng.to_reg(count)
            elif count <= 0:
                return
            eng.wait_ge(weights_in, 96)
            eng.wait_ge(sem, count)

        block = ctx.enter_context(nc.Block())

        @block.sync
        def _(sp):
            sp.dma_start(wqk_raw[:, :], w_qkv).then_inc(weights_in, 16)
            sp.dma_start(gate_raw[:, :], gate_w).then_inc(weights_in, 16)
            sp.dma_start(wproj[:, :], w_proj).then_inc(weights_in, 16)
            for to, row in ((bproj_all, b_proj), (gamma_all, ln_gamma), (beta_all, ln_beta)):
                sp.dma_start(to[:, :], row.rearrange("(o d) -> o d", o=1).broadcast_to([P, D])).then_inc(weights_in, 16)

            def body(t, r, lap):
                if on(t):
                    after(sp, xT_ready, t - 2)
                    sp.dma_start(xin[:, r], x_tiles[t]).then_inc(x_in[r], 16)
                if on(t - 2):
                    after(sp, residuals, 2 * (t - 4))
                    sp.dma_start(xres[:, (r - 2) % 3], x_tiles[t - 2]).then_inc(xres_in[(r - 2) % 3], 16)
                if on(t):
                    stepped = t + 1 if isinstance(t, int) else sp.to_reg(t + 1)
                    after(sp, s_ready, NP * (t - 2))
                    for done, parts in (
                        (h_split, ((q_stack, part_h, 0, (0, 1, 3)), (k_stack, part_h, 1, (0, 2, 4)))),
                        (m_split, ((q_stack, part_m, 0, (2, 5)), (k_stack, part_m, 1, (1, 5)))),
                        (l_split, ((q_stack, part_l, 0, (4,)), (k_stack, part_l, 1, (3,)))),
                    ):
                        sp.wait_ge(done, stepped)
                        if done is h_split and isinstance(t, int) and t == 0:
                            sp.wait_ge(consts_p, 1)
                        for stack, part, which, places in parts:
                            for n in places:
                                sp.dma_start(stack[HD * n:HD * n + HD, r], part[:, which]).then_inc(stacked, 16)
                if on(t - 1):
                    sp.wait_ge(shift_copied, t)
                    sp.dma_start(q_stack[KQ:KQ + 2, (r - 1) % 3], shift_t[:, (r - 1) % 3]).then_inc(shifted, 16)

            run(sp, body)

            with sp.Fori(0, NCH) as c:
                sp.wait_ge(fin_done, c + 1)
                sp.dma_start(out_chunks[c], fin[:, :, :]).then_inc(out_sent, 16)
            sp.wait_ge(out_sent, 16 * NCH + 1)

        @block.gpsimd
        def _(pool):
            pool.memset(ident[:, :], 0.0).then_inc(consts, 1)
            pool.memset(causal_neg[:, :], 0.0).then_inc(consts, 1)
            pool.memset(minus_half[:, :], -0.5).then_inc(consts, 1)
            pool.memset(v_aug[:, :, :, :, HD:32], 0.0).then_inc(consts, 1)
            pool.wait_ge(consts, 4)
            pool.affine_select(out=ident[:, :], in_=ident[:, :], compare_op=ALU.not_equal, fill=1.0, base=0,
                               pattern=[[-1, P]], channel_multiplier=1).then_inc(consts, 1)
            pool.affine_select(out=causal_neg[:, :], in_=causal_neg[:, :], compare_op=ALU.is_ge, fill=NEG, base=0,
                               pattern=[[-1, P]], channel_multiplier=1).then_inc(consts, 1)
            pool.memset(v_aug[:, :, :, :, HD:HD + 1], 1.0).then_inc(consts, 1)
            pool.wait_ge(consts, 7)
            pool.tensor_copy(ident_bf[:, :], ident[:, :]).then_inc(consts, 1)
            pool.wait_ge(weights_in, 96)

            def body(t, r, lap):
                for u in range(NP):
                    s, n = s_unit(t, u)
                    if on(s):
                        wait_apart(pool, exp_done, NP * s + n + 1)
                        for at, step in ((0, T), (2 * T, P)):
                            diag = probs[:, n, at:at + 2 * step].rearrange("p (h q) -> p h q", h=2)[:, :, 0:P]
                            last = pool.affine_select(out=diag, in_=diag, compare_op=ALU.is_ge, fill=0.0, base=0,
                                                      pattern=[[0, 2], [1, P]], channel_multiplier=-1)
                        last.then_inc(masked, 1)
                    if u == 0 and on(t - 4):
                        pool.wait_ge(var_done, t - 3)
                        pool.tensor_tensor(rstd[:, :], var_eps[:, :], minus_half[:, 0:TT], ALU.pow).then_inc(rstd_done, 1)
                    if u == 1 and on(t - 4):
                        pool.wait_ge(yn_done, t - 3)
                        pool.tensor_tensor(yg[:, :, :], yn[:, :, :], gamma_all[:, None, :].broadcast_to([P, TT, D]),
                                           ALU.mult).then_inc(yg_done, 1)
                        pool.wait_ge(yg_done, t - 3)
                        pool.tensor_tensor(ys[:, :, :], yg[:, :, :], x_beta[:, :, :], ALU.add).then_inc(ys_done, 1)
                    if u == 3 and on(t):
                        pool.wait_ge(rest_left, t + 1)
                        wait_apart(pool, stacked, 16 * 12 * t)
                        pool.tensor_copy(part_m[:, :, :], rest[:, :, :]).then_inc(m_split, 1)
                        pool.wait_ge(m_split, t + 1)
                        pool.tensor_tensor(part_l[:, :, :], rest[:, :, :], part_m[:, :, :], ALU.subtract).then_inc(l_split, 1)
                    if u == 3 and on(t - 4):
                        pool.wait_ge(var2_done, t - 3)
                        pool.tensor_tensor(rstd2[:, :], var_eps2[:, :], minus_half[:, 0:TT], ALU.pow).then_inc(rstd2_done, 1)
                    if u == 4 and on(t - 3):
                        pool.wait_ge(xres_in[r], 16 * lap)
                        after(pool, y_ready, t - 3)
                        xr = xres[:, (r - 3) % 3]
                        pool.tensor_tensor(x_bproj[:, :, :], xr, bproj_all[:, None, :].broadcast_to([P, TT, D]),
                                           ALU.add).then_inc(residuals, 1)
                        after(pool, ys_done, t - 3)
                        pool.tensor_tensor(x_beta[:, :, :], xr, beta_all[:, None, :].broadcast_to([P, TT, D]),
                                           ALU.add).then_inc(residuals, 1)
                    if u == 6 and on(t - 4):
                        wait_apart(pool, x2_done, t - 3)
                        pool.tensor_copy(x2_all[:, t - 4], x2[:, (r - 4) % 3]).then_inc(x2_kept, 1)
                        wait_apart(pool, x2T_copied, t - 3)
                        pool.tensor_copy(x2T_all[:, t - 4], x2T[:, (r - 4) % 3]).then_inc(x2T_kept, 1)

            run(pool, body)

            with pool.Fori(0, NCH) as c:
                pool.wait_ge(moe_var, c + 1)
                pool.tensor_tensor(rstd3[:, :], var_eps3[:, :], minus_half[:, :], ALU.pow).then_inc(moe_rstd, 1)

        @block.scalar
        def _(act):
            act.dma_start(w1_sb[:, :, :], w1.rearrange("e d f -> d e f")).then_inc(experts_in, 16)
            act.dma_start(w2_sb[:, :, :, :], w2.rearrange("e (c f) d -> f e c d", f=P)).then_inc(experts_in, 16)
            with nc.allow_non_contiguous_dma(reason="small"):
                act.dma_start(b1_sb[:, :], b1.rearrange("e (c f) -> f (e c)", f=P)).then_inc(experts_in, 16)
            act.dma_start(b2_sb[:, :], b2.rearrange("(o e) d -> o (e d)", o=1)).then_inc(experts_in, 16)
            act.wait_ge(consts, 8)

            def body(t, r, lap):
                for u in range(NP):
                    s, n = s_unit(t, u)
                    if on(s):
                        act.wait_ge(s_ready, NP * s + n + 1)
                        after(act, pv_done, 4 * s - 4 + n // 2 + 1)
                        act.activation(probs[:, n], S[n % 2][:, 0:3 * T], ACT.Exp, scale=SCALE).then_inc(exp_done, 1)
                    if u == 1 and on(t):
                        act.wait_ge(xT_ready, t + 1)
                        act.copy(xT[:, r], G[:, 0:T]).then_inc(xT_copied, 1)
                    if u == 2 and on(t):
                        act.wait_ge(qk_ready, t + 1)
                        after(act, stacked, 16 * 12 * t)
                        act.copy(part_h[:, :, :], G[:, :].rearrange("p (w q) -> p w q", w=2)).then_inc(h_split, 1)
                    if u == 3 and on(t - 3):
                        act.wait_ge(pv_done, 4 * (t - 2))
                        after(act, o_turned, 2 * (t - 3))
                        act.copy(heads_t[:, 2:4], O[:, :].rearrange("p (k q) -> p k q", k=2)).then_inc(o_copied, 1)
                    if u == 3 and on(t):
                        act.wait_ge(v_ready, t + 1)
                        act.copy(v_aug[:, r, :, :, 0:HD],
                                 G[:, 0:T].rearrange("p (i h d) -> p i h d", i=TT, h=H)).then_inc(v_copied, 1)
                    if u == 5 and on(t - 4):
                        act.wait_ge(x2T_ready, t - 3)
                        after(act, x2T_kept, t - 4)
                        act.copy(x2T[:, (r - 4) % 3], G[:, 0:T]).then_inc(x2T_copied, 1)
                    if u == 6 and on(t - 3):
                        act.wait_ge(on_turned, t - 2)
                        act.copy(heads_n_t[:, :], G[:, 0:T]).then_inc(on_copied, 1)
                    if u == 7 and on(t - 1):
                        act.wait_ge(shift_turned, t)
                        after(act, shifted, 16 * (t - 3))
                        act.copy(shift_t[:, (r - 1) % 3], G_bf[0:2 * H * TT, 0:P]).then_inc(shift_copied, 1)
                    if u == 7 and on(t - 2):
                        act.wait_ge(pv_done, 4 * (t - 2) + 2)
                        after(act, o_turned, 2 * (t - 2))
                        act.copy(heads_t[:, 0:2], O[:, :].rearrange("p (k q) -> p k q", k=2)).then_inc(o_copied, 1)

            run(act, body)

            act.wait_ge(diff_done, 1)
            act.activation(exp2[:, :], diff[:, :], ACT.Exp).then_inc(exp2_done, 1)
            act.wait_ge(experts_in, 64)
            with act.Fori(0, NCH) as c:
                for n in range(E * FC):
                    act.wait_ge(h_ready, E * FC * c + n + 1)
                    act.activation(hT[:, n % 4], HB[n % 4], ACT.Gelu, bias=b1_sb[:, n:n + 1]).then_inc(gelu_done, 1)

        @block.vector
        def _(dve):
            dve.memset(k_stack[32:64, :], 1.0).then_inc(consts_p, 1)
            dve.memset(ones_row[:, :], 1.0).then_inc(ones_made, 1)
            for e in range(E):
                dve.memset(expert_no[:, e:e + 1], float(e)).then_inc(numbered, 1)
            dve.wait_ge(weights_in, 96)
            dve.tensor_copy(wqk[:, :, :].rearrange("p w (d h) -> p w d h", d=HD),
                            wqk_raw[:, 0:2 * D].rearrange("p (w h d) -> p w d h", w=2, h=H)).then_inc(consts_v, 1)
            dve.wait_ge(gate_turned, 1)
            dve.tensor_copy(gate_t[:, :], G[:, 0:E]).then_inc(consts_v, 1)

            def body(t, r, lap):
                for u in range(NP):
                    if u == 0 and on(t - 4):
                        dve.wait_ge(y_ready, t - 3)
                        for i in range(TT):
                            dve.bn_stats(stats[:, i], y[:, i]).then_inc(stats_done, 1)
                        for i in range(TT):
                            wait_apart(dve, stats_done, (2 * TT) * (t - 4) + TT + i)
                            dve.bn_aggr(moments[:, i], stats[:, i]).then_inc(stats_done, 1)
                        dve.wait_ge(stats_done, 2 * TT * (t - 3))
                        dve.tensor_scalar(var_eps[:, :], moments[:, :, 1], EPS, None, ALU.add).then_inc(var_done, 1)
                    if u < NM // 2 and on(t - 1):
                        for i in (2 * u, 2 * u + 1):
                            half, h0, nh = M_UNITS[i]
                            dve.wait_ge(m_ready, NM * (t - 1) + i + 1)
                            if i == 0:
                                after(dve, shift_made, t - 3)
                            dve.tensor_reduce(row_max[:, (r - 1) % 3, h0:h0 + nh, half],
                                              M[i % 2][:, :].rearrange("p (h k) -> p h k", h=nh), X, ALU.max).then_inc(m_reduced, 1)
                    if u == 1 and on(t - 4):
                        dve.wait_ge(rstd_done, t - 3)
                        for i in range(TT):
                            last = dve.tensor_scalar(yn[:, i], y[:, i], moments[:, i, 0:1], rstd[:, i:i + 1],
                                                     ALU.subtract, ALU.mult)
                        last.then_inc(yn_done, 1)
                    if u == 2 and on(t):
                        dve.wait_ge(h_split, t + 1)
                        after(dve, l_split, t)
                        dve.tensor_tensor(rest[:, :, :], G[:, :].rearrange("p (w q) -> p w q", w=2), part_h[:, :, :],
                                          ALU.subtract).then_inc(rest_left, 1)
                    if u == 2 and on(t - 4):
                        dve.wait_ge(ys_done, t - 3)
                        for i in range(TT):
                            dve.bn_stats(stats2[:, i], ys[:, i]).then_inc(stats2_done, 1)
                        for i in range(TT):
                            wait_apart(dve, stats2_done, (2 * TT) * (t - 4) + TT + i)
                            dve.bn_aggr(moments2[:, i], stats2[:, i]).then_inc(stats2_done, 1)
                        dve.wait_ge(stats2_done, 2 * TT * (t - 3))
                        dve.tensor_scalar(var_eps2[:, :], moments2[:, :, 1], EPS, None, ALU.add).then_inc(var2_done, 1)
                    if u == 4 and on(t - 4):
                        dve.wait_ge(rstd2_done, t - 3)
                        after(dve, x2_kept, t - 4)
                        for i in range(TT):
                            last = dve.tensor_scalar(x2[:, (r - 4) % 3, i], ys[:, i], moments2[:, i, 0:1], rstd2[:, i:i + 1],
                                                     ALU.subtract, ALU.mult)
                        last.then_inc(x2_done, 1)
                    if u in (4, 5) and on(t - 3):
                        i = u - 4
                        dve.wait_ge(o_turned, 2 * (t - 3) + i + 1)
                        turned = G[:, :].rearrange("p (h c) -> p h c", h=H)
                        dve.reciprocal(inv_sum[:, i], turned[:, :, HD]).then_inc(inverted, 1)
                        dve.wait_ge(inverted, 2 * (t - 3) + i + 1)
                        after(dve, on_turned, t - 3)
                        dve.tensor_tensor(heads[:, i].rearrange("p (h d) -> p h d", h=H), turned[:, :, 0:HD],
                                          inv_sum[:, i, :, None].broadcast_to([P, H, HD]), ALU.mult).then_inc(o_normed, 1)
                    if u == 6 and on(t - 1):
                        dve.wait_ge(m_reduced, NM * t)
                        after(dve, shift_turned, t - 3)
                        b = (r - 1) % 3
                        dve.tensor_scalar(shift[:, b, 0], row_max[:, b], -1.0, None, ALU.mult).then_inc(shift_hi, 1)
                        dve.wait_ge(shift_hi, t)
                        dve.scalar_tensor_tensor(out=shift[:, b, 1], in0=row_max[:, b], scalar=-1.0, in1=shift[:, b, 0],
                                                 op0=ALU.mult, op1=ALU.subtract).then_inc(shift_made, 1)
                    if u == 7 and on(t - 4):
                        dve.wait_ge(gate_ready, t - 3)
                        if on(t - 3):
                            dve.wait_ge(on_copied, t - 2)
                        dve.tensor_copy(logits[:, (r - 4) % 3], G[:, T:T + TT * E].rearrange("p (i e) -> p i e", i=TT)).then_inc(logits_done, 1)
                        wait_apart(dve, logits_done, t - 3)
                        for i in range(TT):
                            dve.max(top_v[:, i], logits[:, (r - 4) % 3, i]).then_inc(top_done, 1)
                        for i in range(TT):
                            wait_apart(dve, top_done, TT * (t - 4) + i + 1)
                            dve.max_index(top_i[:, i], top_v[:, i], logits[:, (r - 4) % 3, i]).then_inc(index_done, 1)
                        dve.wait_ge(index_done, TT * (t - 3))
                        dve.tensor_copy(top_v_all[:, t - 4], top_v[:, :, 0:2]).then_inc(top_kept, 1)
                        dve.tensor_copy(top_i_all[:, t - 4], top_i[:, :, 0:2]).then_inc(top_kept, 1)
                        dve.wait_ge(top_kept, 2 * (t - 3))
                    if u == 7 and on(t - 3):
                        dve.wait_ge(proj_ready, t - 2)
                        dve.wait_ge(residuals, 2 * (t - 3) + 1)
                        after(dve, yn_done, t - 3)
                        dve.tensor_tensor(y[:, :, :], G[:, 0:T].rearrange("p (i d) -> p i d", i=TT), x_bproj[:, :, :],
                                          ALU.add).then_inc(y_ready, 1)

            run(dve, body)

            dve.wait_ge(top_kept, 2 * B)
            tv = top_v_all[:, :, :, :].rearrange("p b i k -> p (b i) k")
            ti = top_i_all[:, :, :, :].rearrange("p b i k -> p (b i) k")
            dve.tensor_tensor(diff[:, :], tv[:, :, 1], tv[:, :, 0], ALU.subtract).then_inc(diff_done, 1)
            dve.wait_ge(exp2_done, 1)
            dve.tensor_scalar(esum[:, :], exp2[:, :], 1.0, None, ALU.add).then_inc(wt, 1)
            dve.wait_ge(wt, 1)
            dve.reciprocal(wgt[:, :, 0], esum[:, :]).then_inc(wt, 1)
            dve.wait_ge(wt, 2)
            dve.tensor_tensor(wgt[:, :, 1], wgt[:, :, 0], exp2[:, :], ALU.mult).then_inc(wt, 1)
            dve.wait_ge(numbered, E)
            for k in range(2):
                dve.wait_ge(wt, 3 + 2 * k)
                dve.tensor_tensor(chosen[:, :, :], ti[:, :, k, None].broadcast_to([P, NT, E]),
                                  expert_no[:, None, :].broadcast_to([P, NT, E]), ALU.is_equal).then_inc(wt, 1)
                dve.wait_ge(wt, 4 + 2 * k)
                dve.tensor_tensor(weights[:, k], chosen[:, :, :], wgt[:, :, k, None].broadcast_to([P, NT, E]),
                                  ALU.mult).then_inc(wt, 1)
            dve.wait_ge(wt, 7)
            dve.tensor_tensor(weights[:, 0], weights[:, 0], weights[:, 1], ALU.add).then_inc(y_used, 2)
            dve.wait_ge(x2_kept, B)
            dve.memset(diff[:, 0:1], 0.0).then_inc(out_sent, 1)
            with dve.Fori(0, NCH) as c:
                for e in range(E):
                    dve.wait_ge(ye_ready, E * c + e + 1)
                    dve.wait_ge(y_used, E * c + e + 2)
                    for i in range(CH):
                        prev = x2_all[:, 2 * c + i // TT, (i % TT) * D:(i % TT) * D + D] if e == 0 else acc[:, i]
                        last = dve.scalar_tensor_tensor(out=acc[:, i], in0=M[e % 2][:, i * D:i * D + D],
                                                        scalar=weights[:, 0, CH * c + i, e:e + 1], in1=prev,
                                                        op0=ALU.mult, op1=ALU.add)
                    last.then_inc(y_used, 1)
                dve.wait_ge(y_used, E * c + E + 2)
                dve.tensor_scalar(clipped[:, :, :], acc[:, :, :], 100.0, -100.0, ALU.min, ALU.max).then_inc(moe, 1)
                dve.wait_ge(moe, 3 * c + 1)
                dve.tensor_tensor(x3[:, :, :], clipped[:, :, :],
                                  x2_all[:, bass.ts(c, 2), :].rearrange("p b (i d) -> p (b i) d", d=D), ALU.add).then_inc(moe, 1)
                dve.wait_ge(moe, 3 * c + 2)
                for i in range(CH):
                    last = dve.bn_stats(stats3[:, i], x3[:, i])
                last.then_inc(moe, 1)
                wait_apart(dve, moe, 3 * c + 3)
                for i in range(CH):
                    last = dve.bn_aggr(moments3[:, i], stats3[:, i])
                last.then_inc(moe_aggr, 1)
                dve.wait_ge(moe_aggr, c + 1)
                dve.tensor_scalar(var_eps3[:, :], moments3[:, :, 1], EPS, None, ALU.add).then_inc(moe_var, 1)
                dve.wait_ge(moe_rstd, c + 1)
                dve.wait_ge(out_sent, 16 * c + 1)
                for i in range(CH):
                    last = dve.tensor_scalar(fin[:, i], x3[:, i], moments3[:, i, 0:1], rstd3[:, i:i + 1],
                                             ALU.subtract, ALU.mult)
                last.then_inc(fin_done, 1)

        @block.tensor
        def _(pe):
            pe.wait_ge(consts, 8)
            pe.wait_ge(weights_in, 96)
            pe.transpose(G[:, 0:E], gate_raw[:, :], ident[0:E, 0:E]).then_inc(gate_turned, 1)
            pe.wait_ge(consts_v, 2)

            def scores(t, r, s, n):
                after(pe, exp_done, NP * s + n - 1)
                if n == 0:
                    pe.wait_ge(shifted, 16 * (s + 1))
                b = (r - (2 if n < NP - 2 else 3)) % 3
                for j in range(2):
                    h = 2 * n + j
                    pe.matmul(S[n % 2][:, j * T:j * T + T], k_stack[0:KQ + 2, b, h, 0:P], q_stack[0:KQ + 2, b, h, :],
                              start=True, stop=True)
                for j in range(2):
                    h = 2 * n + j
                    last = pe.matmul(S[n % 2][:, 2 * T + j * P:2 * T + j * P + P], k_stack[0:KQ + 2, b, h, P:T],
                                     q_stack[0:KQ + 2, b, h, P:T], start=True, stop=True)
                last.then_inc(s_ready, 1)

            def maxima(t, r, i):
                half, h0, nh = M_UNITS[i]
                keys = P * (half + 1)
                if i == 0:
                    pe.wait_ge(stacked, 16 * 12 * t)
                after(pe, m_reduced, NM * (t - 1) + i - 1)
                b = (r - 1) % 3
                bank = M[i % 2]
                for j in range(nh):
                    pe.matmul(bank[:, j * keys:j * keys + keys], q_stack[0:KQ, b, h0 + j, half * P:half * P + P],
                              k_stack[0:KQ, b, h0 + j, 0:keys], start=(j == 0), stop=False, skip_group_check=True)
                diag = bank[:, :].rearrange("p (h k) -> p h k", h=nh)[:, :, keys - P:keys]
                pe.matmul(diag, ident_bf[:, :], causal_neg[:, None, :].broadcast_to([P, nh, P]), start=False, stop=True,
                          skip_group_check=True).then_inc(m_ready, 1)

            def values(t, r, s, k):
                pe.wait_ge(masked, NP * s + 2 * k + 2)
                if k == 0:
                    pe.wait_ge(v_copied, s + 1)
                if k % 2 == 0:
                    after(pe, o_copied, 2 * s + k // 2)
                b = (r - (2 if k < 2 else 3)) % 3
                at = (k % 2) * T
                for j in range(4):
                    h = 4 * k + j
                    pe.matmul(O[32 * j:32 * j + 32, at:at + T], v_aug[:, b, 0, h], probs[:, h // 2, (h % 2) * T:(h % 2) * T + T],
                              start=True, stop=False, skip_group_check=True)
                for j in range(4):
                    h = 4 * k + j
                    last = pe.matmul(O[32 * j:32 * j + 32, at + P:at + T], v_aug[:, b, 1, h],
                                     probs[:, h // 2, 2 * T + (h % 2) * P:2 * T + (h % 2) * P + P],
                                     start=False, stop=True, skip_group_check=True)
                last.then_inc(pv_done, 1)

            def body(t, r, lap):
                for u in range(NP):
                    s, n = s_unit(t, u)
                    if on(s):
                        scores(t, r, s, n)
                    if u == 1 and on(t):
                        if on(t - 4):
                            pe.wait_ge(y_ready, t - 3)
                        elif on(t - 2):
                            pe.wait_ge(shift_copied, t - 1)
                        elif on(t - 1):
                            pe.wait_ge(v_copied, t)
                        pe.wait_ge(x_in[r], 16 * (lap + 1))
                        for i in range(TT):
                            last = pe.transpose(G[:, i * P:i * P + P], xin[:, r, i], ident[:, :])
                        last.then_inc(xT_ready, 1)
                    if u == 2 and on(t):
                        pe.wait_ge(xT_copied, t + 1)
                        for w in range(2):
                            last = pe.matmul(G[:, w * T:w * T + T], wqk[:, w], xT[:, r], start=True, stop=True)
                        last.then_inc(qk_ready, 1)
                    if u == 3 and on(t):
                        pe.wait_ge(h_split, t + 1)
                        pe.wait_ge(rest_left, t + 1)
                        for i in range(TT):
                            last = pe.matmul(G[:, i * P:i * P + P], xT[:, r, i * P:i * P + P], wqk_raw[:, 2 * D:3 * D],
                                             start=True, stop=True)
                        last.then_inc(v_ready, 1)
                    if u < NM // 2 and on(t - 1):
                        maxima(t, r, 2 * u)
                        maxima(t, r, 2 * u + 1)
                    if pv_quad(t, u) and on(pv_quad(t, u)[0]):
                        values(t, r, *pv_quad(t, u))
                    if u in (4, 5) and on(t - 3):
                        i = u - 4
                        pe.wait_ge(o_copied, 2 * (t - 2))
                        if on(t):
                            pe.wait_ge(v_copied, t + 1)
                        elif i == 0 and on(t - 4):
                            pe.wait_ge(y_ready, t - 3)
                        after(pe, o_normed, 2 * (t - 3) + i)
                        for k in range(4):
                            last = pe.transpose(G[:, k * P:k * P + P], heads_t[:, k, i * P:i * P + P], ident[:, :])
                        last.then_inc(o_turned, 1)
                    if u == 5 and on(t - 4):
                        pe.wait_ge(x2_done, t - 3)
                        if on(t - 3):
                            pe.wait_ge(o_normed, 2 * (t - 2))
                        else:
                            pe.wait_ge(y_ready, t - 3)
                        for i in range(TT):
                            last = pe.transpose(G[:, i * P:i * P + P], x2[:, (r - 4) % 3, i], ident[:, :])
                        last.then_inc(x2T_ready, 1)
                    if u == 6 and on(t - 4):
                        pe.wait_ge(x2T_copied, t - 3)
                        for i in range(TT):
                            last = pe.matmul(G[:, T + i * E:T + i * E + E], x2T[:, (r - 4) % 3, i * P:i * P + P], gate_t[:, :],
                                             start=True, stop=True)
                        last.then_inc(gate_ready, 1)
                    if u == 6 and on(t - 3):
                        pe.wait_ge(o_normed, 2 * (t - 2))
                        for i in range(TT):
                            last = pe.transpose(G[:, i * P:i * P + P], heads[:, i], ident[:, :])
                        last.then_inc(on_turned, 1)
                    if u == 7 and on(t - 1):
                        wait_apart(pe, shift_made, t)
                        if on(t - 4):
                            pe.wait_ge(logits_done, t - 3)
                        if on(t - 3):
                            pe.wait_ge(on_copied, t - 2)
                        elif on(t):
                            pe.wait_ge(v_copied, t + 1)
                        pe.transpose(G_bf[0:2 * H * TT, 0:P], shift[:, (r - 1) % 3].rearrange("p w h i -> p (w h i)"),
                                     ident_bf[:, :]).then_inc(shift_turned, 1)
                    if u == 7 and on(t - 3):
                        pe.wait_ge(on_copied, t - 2)
                        if on(t - 4):
                            pe.wait_ge(logits_done, t - 3)
                        if on(t - 1):
                            pe.wait_ge(shift_copied, t)
                        for i in range(TT):
                            last = pe.matmul(G[:, i * P:i * P + P], heads_n_t[:, i * P:i * P + P], wproj[:, :],
                                             start=True, stop=True)
                        last.then_inc(proj_ready, 1)

            run(pe, body)

            pe.wait_ge(x2T_kept, B)
            pe.wait_ge(experts_in, 64)
            pe.wait_ge(ones_made, 1)
            pe.wait_ge(exp_done, NP * B)
            with pe.Fori(0, NCH) as c:
                def first_layer(e):
                    for f in range(FC):
                        pe.matmul(HB[(e * FC + f) % 4], w1_sb[:, e, f * P:f * P + P], x2T_all[:, bass.ts(c, 2), :],
                                  start=True, stop=True).then_inc(h_ready, 1)

                first_layer(0)
                for e in range(E):
                    if e + 1 < E:
                        first_layer(e + 1)
                    pe.wait_ge(y_used, E * c + e + 1)
                    pe.matmul(M[e % 2][:, :], ones_row[:, :], b2_sb[:, e * D:e * D + D][:, None, :].broadcast_to([1, CH, D]),
                              start=True, stop=False, skip_group_check=True)
                    for f in range(FC):
                        n = e * FC + f
                        pe.wait_ge(gelu_done, E * FC * c + n + 1)
                        for i in range(CH):
                            last = pe.matmul(M[e % 2][:, i * D:i * D + D], hT[:, n % 4, i * P:i * P + P], w2_sb[:, e, f],
                                             start=False, stop=(f == FC - 1), skip_group_check=True)
                    last.then_inc(ye_ready, 1)


_INS = ['L0_attn_target', 'L0_attn_w_qkv', 'L0_attn_w_proj', 'L0_attn_b_proj', 'L0_attn_ln_gamma', 'L0_attn_ln_beta',
        'L0_ffn_gate_w', 'L0_ffn_w1', 'L0_ffn_b1', 'L0_ffn_w2', 'L0_ffn_b2']
_OUTS = [((16, 256, 128), 'float32')]


def kernel(**inputs):
    import numpy as _np
    import concourse.bacc as _bacc
    from concourse import mybir as _mybir
    from concourse.bass_utils import run_bass_kernel_spmd as _run

    nc = _bacc.Bacc("TRN2", target_bir_lowering=False, num_devices=1)
    arrays, args = {}, []
    for name in _INS:
        a = _np.ascontiguousarray(inputs[name])
        arrays[f"in_{name}_dram"] = a
        args.append(nc.dram_tensor(f"in_{name}_dram", a.shape, _mybir.dt.from_np(a.dtype), kind="ExternalInput").ap())
    for i, (shape, dtype) in enumerate(_OUTS):
        dt = _mybir.dt.from_np(_np.dtype(dtype))
        args.append(nc.dram_tensor(f"out_{i}_dram", shape, dt, kind="ExternalOutput").ap())
    transformer_layer(nc, *args)
    r = _run(nc, [arrays], core_ids=[0])
    got = tuple(r.results[0][f"out_{i}_dram"] for i in range(len(_OUTS)))
    return got[0]
```

```python
from contextlib import ExitStack

import concourse.bass as bass
from concourse import mybir

F32 = mybir.dt.float32
BF16 = mybir.dt.bfloat16
U32 = mybir.dt.uint32
I32 = mybir.dt.int32
ALU = mybir.AluOpType
ACT = mybir.ActivationFunctionType
X = mybir.AxisListType.X

P = 128
H = 16
EPS = 1e-5
NEG = -1e30


def after(eng, sem, count):
    if not isinstance(count, int) or count > 0:
        eng.wait_ge(sem, count)


def transformer_layer(nc, x, w_qkv, w_proj, b_proj, ln_gamma, ln_beta, gate_w, w1, b1, w2, b2, out):
    B, T, D = x.shape
    E, _, F = w1.shape
    HD = D // H
    SCALE = float(HD) ** -0.5
    TT = T // P
    NT = B * TT
    FC = F // P
    NP = H // 2
    SHIFT = 96
    assert D == P and T == 2 * P and H * HD == P
    N = B * T
    REGION = N + P
    ROW = D + 1
    XR = 6
    TILES = -(-(2 * N // P + E - 1) // XR) * XR

    def on(s):
        return not isinstance(s, int) or 0 <= s < B

    def is_tile(s):
        return not isinstance(s, int) or 0 <= s < TILES

    sorted_rows = nc.dram_tensor("sorted_rows", (E * REGION + P, ROW), F32, kind="Internal").ap()
    results = nc.dram_tensor("results", (2 * N, D), F32, kind="Internal").ap()

    x_tiles = x.rearrange("b (i p) d -> b p i d", p=P)
    out_chunks = out.rearrange("(c b) (i p) d -> c p (b i) d", b=2, p=P)

    with ExitStack() as ctx:
        def sb(name, shape, dt=F32):
            return ctx.enter_context(nc.sbuf_tensor(name, shape, dt))

        def ps(name, shape, dt=F32):
            return ctx.enter_context(nc.psum_tensor(name, shape, dt))

        def sem(name):
            return ctx.enter_context(nc.semaphore(name))

        ident = sb("ident", [P, P])
        ident_bf = sb("ident_bf", [P, P], BF16)
        causal_neg = sb("causal_neg", [P, P], BF16)
        minus_half = sb("minus_half", [P, 4])
        expert_no = sb("expert_no", [P, E])
        wqk_raw = sb("wqk_raw", [P, 3 * D])
        wqk = sb("wqk", [P, 2, D])
        wproj = sb("wproj", [P, D])
        gate_raw = sb("gate_raw", [E, D])
        gate_t = sb("gate_t", [P, E])
        bproj_all = sb("bproj_all", [P, D])
        gamma_all = sb("gamma_all", [P, D])
        beta_all = sb("beta_all", [P, D])
        layer1 = sb("layer1", [P, E * (F + FC)])
        layer2 = sb("layer2", [P, E * F])
        bias2 = sb("bias2", [P, E * D])
        earlier = sb("earlier", [P, P], BF16)
        ones_bf = sb("ones_bf", [P, P], BF16)
        region_at = sb("region_at", [P, E])
        tile_no = sb("tile_no", [P, 1])
        tile_no_i = sb("tile_no_i", [P, 1], I32)
        place = sb("place", [P, B, TT, 2], U32)
        pad = sb("pad", [P, ROW])
        xin = sb("xin", [P, 3, TT, D])
        xres = sb("xres", [P, 3, TT, D])
        xT = sb("xT", [P, 3, T])
        part_h = sb("part_h", [P, 2, T], BF16)
        part_m = sb("part_m", [P, 2, T], BF16)
        part_l = sb("part_l", [P, 2, T], BF16)
        rest = sb("rest", [P, 2, T])
        v_aug = sb("v_aug", [P, 3, TT, H, 32])
        q_stack = sb("q_stack", [P, 3, H, T], BF16)
        k_stack = sb("k_stack", [P, 3, H, T], BF16)
        row_max = sb("row_max", [P, 3, H, TT])
        shift = sb("shift", [P, 3, 2, H, TT], BF16)
        shift_t = sb("shift_t", [2 * H * TT, 3, P], BF16)
        probs = sb("probs", [P, NP, 3 * T])
        heads_t = sb("heads_t", [P, 4, T])
        inv_sum = sb("inv_sum", [P, TT, H])
        heads = sb("heads", [P, TT, D])
        heads_n_t = sb("heads_n_t", [P, T])
        x_bproj = sb("x_bproj", [P, TT, D])
        x_beta = sb("x_beta", [P, TT, D])
        y = sb("y", [P, TT, D])
        stats = sb("stats", [P, TT, 6])
        moments = sb("moments", [P, TT, 2])
        var_eps = sb("var_eps", [P, TT])
        rstd = sb("rstd", [P, TT])
        yn = sb("yn", [P, TT, D])
        yg = sb("yg", [P, TT, D])
        ys = sb("ys", [P, TT, D])
        stats2 = sb("stats2", [P, TT, 6])
        moments2 = sb("moments2", [P, TT, 2])
        var_eps2 = sb("var_eps2", [P, TT])
        rstd2 = sb("rstd2", [P, TT])
        x2 = sb("x2", [P, 3, 2, TT, ROW])
        x2_all = sb("x2_all", [P, B, TT * D])
        x2T = sb("x2T", [P, 3, T])
        logits = sb("logits", [P, 3, TT, E])
        top_v = sb("top_v", [P, TT, 8])
        top_i = sb("top_i", [P, TT, 8], U32)
        top_v_all = sb("top_v_all", [P, B, TT, 2])
        top_i_f = sb("top_i_f", [P, TT, 2])
        chosen = sb("chosen", [P, TT, 2, E])
        both = sb("both", [P, TT, E], BF16)
        seen = sb("seen", [P, E], BF16)
        row_of = sb("row_of", [P, TT, E])
        row_chosen = sb("row_chosen", [P, TT * 2, E])
        row_f = sb("row_f", [P, TT * 2])
        row_no = sb("row_no", [P, 3 * TT * 2], U32)
        pad_row = sb("pad_row", [P, E], I32)
        rounded = sb("rounded", [P, E], I32)
        tiles_i = sb("tiles_i", [P, E], I32)
        tiles = sb("tiles", [P, E])
        ones_e = sb("ones_e", [P, E])
        tiles_end = sb("tiles_end", [P, E])
        ended = sb("ended", [P, E])
        skip = sb("skip", [P, E])
        skipped = sb("skipped", [P, E])
        n_ended = sb("n_ended", [P, 1])
        n_skipped = sb("n_skipped", [P, 1])
        tile_f = sb("tile_f", [P, 2])
        tile_i = sb("tile_i", [1, 2, P], I32)

        CH = 2 * TT
        NCH = NT // CH
        diff = sb("diff", [P, NT])
        exp2 = sb("exp2", [P, NT])
        esum = sb("esum", [P, NT])
        wgt = sb("wgt", [P, NT, 2])
        rows = sb("rows", [P, XR, ROW])
        rows_t = sb("rows_t", [P, 2, P])
        now1 = sb("now1", [P, 3, F + FC])
        hT = sb("hT", [P, 2, FC, P])
        y_rows = sb("y_rows", [P, XR, D])
        late = q_stack[:, :, :, :].rearrange("p r h q -> p (r h q)").bitcast(F32)
        got = late[:, 0:4 * CH * D].rearrange("p (c k i d) -> p c k i d", c=2, k=2, d=D)
        first, acc, summed, clipped, x3, fin = (
            late[:, (4 + n) * CH * D:(5 + n) * CH * D].rearrange("p (i d) -> p i d", d=D) for n in range(6))
        stats3 = sb("stats3", [P, CH, 6])
        moments3 = sb("moments3", [P, CH, 2])
        var_eps3 = sb("var_eps3", [P, CH])
        rstd3 = sb("rstd3", [P, CH])

        S = [ps(f"S{i}", [P, 1024]) for i in range(2)]
        M = [ps(f"M{i}", [P, 512]) for i in range(2)]
        O = ps("O", [P, 512])
        G = ps("G", [P, 512])
        G_bf = G[:, :].bitcast(BF16)
        hidden = [S[i // FC][:, (i % FC) * 512:(i % FC) * 512 + P] for i in range(2 * FC)]

        weights_in = sem("weights_in")
        experts_in = sem("experts_in")
        consts = sem("consts")
        consts_v = sem("consts_v")
        consts_p = sem("consts_p")
        gate_turned = sem("gate_turned")
        x_in = [sem(f"x_in{i}") for i in range(3)]
        xres_in = [sem(f"xres_in{i}") for i in range(3)]
        stacked = sem("stacked")
        shifted = sem("shifted")
        xT_ready = sem("xT_ready")
        xT_copied = sem("xT_copied")
        qk_ready = sem("qk_ready")
        h_split = sem("h_split")
        rest_left = sem("rest_left")
        m_split = sem("m_split")
        l_split = sem("l_split")
        v_ready = sem("v_ready")
        v_copied = sem("v_copied")
        m_ready = sem("m_ready")
        m_reduced = sem("m_reduced")
        shift_hi = sem("shift_hi")
        shift_made = sem("shift_made")
        shift_turned = sem("shift_turned")
        shift_copied = sem("shift_copied")
        s_ready = sem("s_ready")
        exp_done = sem("exp_done")
        masked = sem("masked")
        pv_done = sem("pv_done")
        o_copied = sem("o_copied")
        o_turned = sem("o_turned")
        inverted = sem("inverted")
        o_normed = sem("o_normed")
        on_turned = sem("on_turned")
        on_copied = sem("on_copied")
        proj_ready = sem("proj_ready")
        residuals = sem("residuals")
        y_ready = sem("y_ready")
        stats_done = sem("stats_done")
        var_done = sem("var_done")
        rstd_done = sem("rstd_done")
        yn_done = sem("yn_done")
        yg_done = sem("yg_done")
        ys_done = sem("ys_done")
        stats2_done = sem("stats2_done")
        var2_done = sem("var2_done")
        rstd2_done = sem("rstd2_done")
        x2_done = sem("x2_done")
        x2_kept = sem("x2_kept")
        x2T_ready = sem("x2T_ready")
        x2T_copied = sem("x2T_copied")
        x2_twice = sem("x2_twice")
        placed = sem("placed")
        gate_ready = sem("gate_ready")
        logits_done = sem("logits_done")
        top_done = sem("top_done")
        index_done = sem("index_done")
        top_kept = sem("top_kept")
        numbered = sem("numbered")
        iotas = sem("iotas")
        chosen_done = sem("chosen_done")
        both_done = sem("both_done")
        seen_done = sem("seen_done")
        rank_ready = sem("rank_ready")
        rank_read = sem("rank_read")
        row_done = sem("row_done")
        row_ready = sem("row_ready")
        scattered = [sem(f"scattered{i}") for i in range(3)]
        counts_ready = sem("counts_ready")
        table = sem("table")
        pad_rows_done = sem("pad_rows_done")
        tile_f_done = sem("tile_f_done")
        tile_turned = sem("tile_turned")
        tile_i_done = sem("tile_i_done")
        padded = sem("padded")
        rows_in = [sem(f"rows_in{i}") for i in range(XR)]
        sent = [sem(f"sent{i}") for i in range(XR)]
        rows_turned = sem("rows_turned")
        rows_copied = sem("rows_copied")
        layer_now = sem("layer_now")
        got_in = [sem(f"got_in{i}") for i in range(2)]
        first_done = sem("first_done")
        diff_done = sem("diff_done")
        exp2_done = sem("exp2_done")
        wt = sem("wt")
        h_ready = sem("h_ready")
        gelu_done = sem("gelu_done")
        y_biased = sem("y_biased")
        layer2_done = sem("layer2_done")
        moe = sem("moe")
        moe_aggr = sem("moe_aggr")
        moe_var = sem("moe_var")
        moe_rstd = sem("moe_rstd")
        fin_done = sem("fin_done")
        out_sent = sem("out_sent")

        FIRST, LAST = 5, 5 + (B - 5) // 3 * 3

        def run(eng, body):
            for t in range(FIRST):
                body(t, t % 3, t // 3)
            with eng.Fori(0, (LAST - FIRST) // 3) as i:
                for k in range(3):
                    body(i * 3 + (FIRST + k), (FIRST + k) % 3, i + (FIRST + k) // 3)
            for t in range(LAST, B + 5):
                body(t, t % 3, t // 3)

        def run_tiles(eng, body):
            for s in range(XR):
                body(s, s % XR, s // XR)
            with eng.Fori(0, TILES // XR - 1) as i:
                for k in range(XR):
                    body(i * XR + (XR + k), k, i + 1)
            for s in range(TILES, TILES + 2):
                body(s, s % XR, s // XR)

        M_UNITS = []
        for p in range(NP):
            M_UNITS.append((1, 2 * p, 2))
            if p % 2:
                M_UNITS.append((0, 2 * p - 2, 4))
        NM = len(M_UNITS)

        def s_unit(t, u):
            return (t - 2, u - 2) if u >= 2 else (t - 3, u + NP - 2)

        def pv_quad(t, u):
            return {1: (t - 3, 2), 3: (t - 3, 3), 5: (t - 2, 0), 7: (t - 2, 1)}.get(u)

        def wait_apart(eng, sem, count, *more):
            if not isinstance(count, int):
                count = eng.to_reg(count)
            elif count <= 0:
                return
            eng.wait_ge(weights_in, 96)
            for s in (sem, *more):
                eng.wait_ge(s, count)

        block = ctx.enter_context(nc.Block())

        @block.sync
        def _(sp):
            sp.dma_start(wqk_raw[:, :], w_qkv).then_inc(weights_in, 16)
            sp.dma_start(gate_raw[:, :], gate_w).then_inc(weights_in, 16)
            sp.dma_start(wproj[:, :], w_proj).then_inc(weights_in, 16)
            for to, row in ((bproj_all, b_proj), (gamma_all, ln_gamma), (beta_all, ln_beta)):
                sp.dma_start(to[:, :], row.rearrange("(o d) -> o d", o=1).broadcast_to([P, D])).then_inc(weights_in, 16)

            def body(t, r, lap):
                if on(t):
                    after(sp, xT_ready, t - 2)
                    sp.dma_start(xin[:, r], x_tiles[t]).then_inc(x_in[r], 16)
                if on(t - 2):
                    after(sp, residuals, 2 * (t - 4))
                    sp.dma_start(xres[:, (r - 2) % 3], x_tiles[t - 2]).then_inc(xres_in[(r - 2) % 3], 16)
                if on(t):
                    stepped = t + 1 if isinstance(t, int) else sp.to_reg(t + 1)
                    after(sp, s_ready, NP * (t - 2))
                    for done, parts in (
                        (h_split, ((q_stack, part_h, 0, (0, 1, 3)), (k_stack, part_h, 1, (0, 2, 4)))),
                        (m_split, ((q_stack, part_m, 0, (2, 5)), (k_stack, part_m, 1, (1, 5)))),
                        (l_split, ((q_stack, part_l, 0, (4,)), (k_stack, part_l, 1, (3,)))),
                    ):
                        sp.wait_ge(done, stepped)
                        if done is h_split and isinstance(t, int) and t == 0:
                            sp.wait_ge(consts_p, 3)
                        for stack, part, which, places in parts:
                            for n in places:
                                sp.dma_start(stack[HD * n:HD * n + HD, r], part[:, which]).then_inc(stacked, 16)
                if on(t - 1):
                    sp.wait_ge(shift_copied, t)
                    sp.dma_start(q_stack[SHIFT:SHIFT + 2, (r - 1) % 3], shift_t[:, (r - 1) % 3]).then_inc(shifted, 16)

            run(sp, body)

            sp.wait_ge(iotas, 6)
            sp.dma_start(sorted_rows[bass.ds(E * REGION, P)], pad[:, :]).then_inc(padded, 16)
            sp.wait_ge(pad_rows_done, 1)
            with sp.Fori(0, E) as e:
                at = sp.value_load(pad_row[0:1, bass.ds(e, 1)], min_val=0, max_val=E * REGION)
                sp.dma_start(sorted_rows[bass.ds(at, P)], pad[:, :]).then_inc(padded, 16)
            sp.wait_ge(tile_i_done, 1)
            sp.wait_ge(padded, 16 * (E + 1))
            for i in range(3):
                sp.wait_ge(scattered[i], 16 * 2 * TT * len(range(i, B, 3)))

            def load_rows(s, q, turn):
                if is_tile(s):
                    at = sp.value_load(tile_i[0:1, 1, bass.ds(s, 1)], min_val=0, max_val=E * REGION)
                    after(sp, sent[q], 16 * turn)
                    sp.dma_start(rows[:, q], sorted_rows[bass.ds(at, P)]).then_inc(rows_in[q], 16)

            run_tiles(sp, load_rows)

            for q in range(XR):
                sp.wait_ge(sent[q], 16 * (TILES // XR))
            by_chunk = results.rearrange("(k c i p) d -> c k p i d", k=2, p=P, i=CH)
            for c in range(NCH):
                after(sp, moe, 5 * (c - 2) + 1)
                for k in range(2):
                    sp.dma_start(got[:, c % 2, k], by_chunk[c, k]).then_inc(got_in[c % 2], 16)
                if c > 0:
                    sp.wait_ge(fin_done, c)
                    sp.dma_start(out_chunks[c - 1], fin[:, :, :]).then_inc(out_sent, 16)
            sp.wait_ge(fin_done, NCH)
            sp.dma_start(out_chunks[NCH - 1], fin[:, :, :]).then_inc(out_sent, 16)
            sp.wait_ge(out_sent, 16 * NCH)

        @block.gpsimd
        def _(pool):
            pool.memset(ident[:, :], 0.0).then_inc(consts, 1)
            pool.memset(causal_neg[:, :], 0.0).then_inc(consts, 1)
            pool.memset(minus_half[:, :], -0.5).then_inc(consts, 1)
            pool.memset(v_aug[:, :, :, :, HD:32], 0.0).then_inc(consts, 1)
            pool.wait_ge(consts, 4)
            pool.affine_select(out=ident[:, :], in_=ident[:, :], compare_op=ALU.not_equal, fill=1.0, base=0,
                               pattern=[[-1, P]], channel_multiplier=1).then_inc(consts, 1)
            pool.affine_select(out=causal_neg[:, :], in_=causal_neg[:, :], compare_op=ALU.is_ge, fill=NEG, base=0,
                               pattern=[[-1, P]], channel_multiplier=1).then_inc(consts, 1)
            pool.memset(v_aug[:, :, :, :, HD:HD + 1], 1.0).then_inc(consts, 1)
            pool.wait_ge(consts, 7)
            pool.tensor_copy(ident_bf[:, :], ident[:, :]).then_inc(consts, 1)
            pool.memset(k_stack[0:SHIFT, :, :, :].rearrange("p r h q -> p (r h q)").bitcast(U32), 0).then_inc(consts_p, 1)
            pool.memset(earlier[:, :], 1.0).then_inc(iotas, 1)
            pool.memset(pad[:, :], 0.0).then_inc(iotas, 1)
            pool.iota(place[:, :, :, :].rearrange("p b i k -> p (b i) k"), pattern=[[P, NT], [N, 2]], base=0,
                      channel_multiplier=1).then_inc(iotas, 1)
            pool.iota(tile_no_i[:, :], pattern=[[0, 1]], base=0, channel_multiplier=1).then_inc(iotas, 1)
            pool.wait_ge(iotas, 4)
            pool.affine_select(out=earlier[:, :], in_=earlier[:, :], compare_op=ALU.is_gt, fill=0.0, base=0,
                               pattern=[[1, P]], channel_multiplier=-1).then_inc(iotas, 1)
            pool.memset(pad[:, D:ROW].bitcast(U32), 2 * N).then_inc(iotas, 1)
            pool.wait_ge(consts_p, 3)
            pool.wait_ge(weights_in, 96)

            def body(t, r, lap):
                for u in range(NP):
                    s, n = s_unit(t, u)
                    if on(s):
                        wait_apart(pool, exp_done, NP * s + n + 1)
                        for at, step in ((0, T), (2 * T, P)):
                            diag = probs[:, n, at:at + 2 * step].rearrange("p (h q) -> p h q", h=2)[:, :, 0:P]
                            last = pool.affine_select(out=diag, in_=diag, compare_op=ALU.is_ge, fill=0.0, base=0,
                                                      pattern=[[0, 2], [1, P]], channel_multiplier=-1)
                        last.then_inc(masked, 1)
                    if u == 0 and on(t - 4):
                        pool.wait_ge(var_done, t - 3)
                        pool.tensor_tensor(rstd[:, :], var_eps[:, :], minus_half[:, 0:TT], ALU.pow).then_inc(rstd_done, 1)
                    if u == 1 and on(t - 4):
                        pool.wait_ge(yn_done, t - 3)
                        pool.tensor_tensor(yg[:, :, :], yn[:, :, :], gamma_all[:, None, :].broadcast_to([P, TT, D]),
                                           ALU.mult).then_inc(yg_done, 1)
                        pool.wait_ge(yg_done, t - 3)
                        pool.tensor_tensor(ys[:, :, :], yg[:, :, :], x_beta[:, :, :], ALU.add).then_inc(ys_done, 1)
                    if u == 3 and on(t):
                        after(pool, stacked, 16 * 12 * t)
                        pool.wait_ge(m_split, t + 1)
                        pool.tensor_tensor(part_l[:, :, :], rest[:, :, :], part_m[:, :, :], ALU.subtract).then_inc(l_split, 1)
                    if u == 3 and on(t - 4):
                        pool.wait_ge(var2_done, t - 3)
                        pool.tensor_tensor(rstd2[:, :], var_eps2[:, :], minus_half[:, 0:TT], ALU.pow).then_inc(rstd2_done, 1)
                    if u == 4 and on(t - 3):
                        pool.wait_ge(xres_in[r], 16 * lap)
                        after(pool, y_ready, t - 3)
                        xr = xres[:, (r - 3) % 3]
                        pool.tensor_tensor(x_bproj[:, :, :], xr, bproj_all[:, None, :].broadcast_to([P, TT, D]),
                                           ALU.add).then_inc(residuals, 1)
                        after(pool, ys_done, t - 3)
                        pool.tensor_tensor(x_beta[:, :, :], xr, beta_all[:, None, :].broadcast_to([P, TT, D]),
                                           ALU.add).then_inc(residuals, 1)
                    if u in (1, 3, 5, 6) and on(t - 5):
                        n = (1, 3, 5, 6).index(u)
                        q = (r - 5) % 3
                        if n == 0:
                            wait_apart(pool, placed, t - 4, x2_twice, row_ready)
                        pool.indirect_dma_start(sorted_rows, bass.IndirectOffsetOnAxis(
                            ap=row_no[:, q * 2 * TT + n:q * 2 * TT + n + 1], axis=0), x2[:, q, n % 2, n // 2], None).then_inc(scattered[q], 16)

            run(pool, body)

            def send(s, q, turn):
                if is_tile(s - 2):
                    q = (q - 2) % XR
                    wait_apart(pool, y_biased, s - 1)
                    pool.indirect_dma_start(results, bass.IndirectOffsetOnAxis(ap=rows[:, q, D:ROW].bitcast(U32), axis=0),
                                            y_rows[:, q], None, bounds_check=2 * N - 1, oob_is_err=False).then_inc(sent[q], 16)

            run_tiles(pool, send)

            for c in range(NCH):
                pool.wait_ge(moe_var, c + 1)
                pool.tensor_tensor(rstd3[:, :], var_eps3[:, :], minus_half[:, :], ALU.pow).then_inc(moe_rstd, 1)

        @block.scalar
        def _(act):
            by_expert = layer1[:, :].rearrange("p (e n) -> p e n", e=E)
            act.dma_start(by_expert[:, :, 0:F], w1.rearrange("e d f -> d e f")).then_inc(experts_in, 16)
            act.dma_start(layer2[:, :].rearrange("p (e c d) -> p e c d", e=E, c=FC),
                          w2.rearrange("e (c f) d -> f e c d", f=P)).then_inc(experts_in, 16)
            with nc.allow_non_contiguous_dma(reason="small"):
                for c in range(FC):
                    act.dma_start(by_expert[:, :, F + c], b1[:, c * P:c * P + P].rearrange("e f -> f e")).then_inc(experts_in, 16)
            act.dma_start(bias2[:, :], b2.rearrange("(o e) d -> o (e d)", o=1).broadcast_to([P, E * D])).then_inc(experts_in, 16)
            act.wait_ge(consts, 8)

            def body(t, r, lap):
                for u in range(NP):
                    s, n = s_unit(t, u)
                    if on(s):
                        act.wait_ge(s_ready, NP * s + n + 1)
                        after(act, pv_done, 4 * s - 4 + n // 2 + 1)
                        act.activation(probs[:, n], S[n % 2][:, 0:3 * T], ACT.Exp, scale=SCALE).then_inc(exp_done, 1)
                    if u == 1 and on(t):
                        act.wait_ge(xT_ready, t + 1)
                        act.copy(xT[:, r], G[:, 0:T]).then_inc(xT_copied, 1)
                    if u == 2 and on(t):
                        act.wait_ge(qk_ready, t + 1)
                        after(act, stacked, 16 * 12 * t)
                        act.copy(part_h[:, :, :], G[:, :].rearrange("p (w q) -> p w q", w=2)).then_inc(h_split, 1)
                    if u == 2 and on(t):
                        act.wait_ge(rest_left, t + 1)
                        act.copy(part_m[:, :, :], rest[:, :, :]).then_inc(m_split, 1)
                    if u == 3 and on(t - 3):
                        act.wait_ge(pv_done, 4 * (t - 2))
                        after(act, o_turned, 2 * (t - 3))
                        act.copy(heads_t[:, 2:4], O[:, :].rearrange("p (k q) -> p k q", k=2)).then_inc(o_copied, 1)
                    if u == 3 and on(t):
                        act.wait_ge(v_ready, t + 1)
                        act.copy(v_aug[:, r, :, :, 0:HD],
                                 G[:, 0:T].rearrange("p (i h d) -> p i h d", i=TT, h=H)).then_inc(v_copied, 1)
                    if u == 5 and on(t - 4):
                        act.wait_ge(x2T_ready, t - 3)
                        act.copy(x2T[:, (r - 4) % 3], G[:, 0:T]).then_inc(x2T_copied, 1)
                        act.wait_ge(x2_done, t - 3)
                        act.copy(x2[:, (r - 4) % 3, 1, :, 0:D], x2[:, (r - 4) % 3, 0, :, 0:D]).then_inc(x2_twice, 1)
                    if u == 6 and on(t - 3):
                        act.wait_ge(on_turned, t - 2)
                        act.copy(heads_n_t[:, :], G[:, 0:T]).then_inc(on_copied, 1)
                    if u == 6 and on(t - 4):
                        act.copy(x2_all[:, t - 4].rearrange("p (i d) -> p i d", i=TT), x2[:, (r - 4) % 3, 0, :, 0:D]).then_inc(x2_kept, 1)
                    if u == 7 and on(t - 1):
                        act.wait_ge(shift_turned, t)
                        after(act, shifted, 16 * (t - 3))
                        act.copy(shift_t[:, (r - 1) % 3], G_bf[0:2 * H * TT, 0:P]).then_inc(shift_copied, 1)
                    if u == 7 and on(t - 2):
                        act.wait_ge(pv_done, 4 * (t - 2) + 2)
                        after(act, o_turned, 2 * (t - 2))
                        act.copy(heads_t[:, 0:2], O[:, :].rearrange("p (k q) -> p k q", k=2)).then_inc(o_copied, 1)

            run(act, body)

            act.wait_ge(diff_done, 1)
            act.activation(exp2[:, :], diff[:, :], ACT.Exp).then_inc(exp2_done, 1)

            def layers(s, q, turn):
                if is_tile(s):
                    act.wait_ge(rows_turned, s + 1)
                    after(act, h_ready, 2 * s - 2)
                    act.copy(rows_t[:, q % 2], (G, O)[q % 2][:, 0:P]).then_inc(rows_copied, 1)
                if is_tile(s - 1):
                    after(act, layer2_done, s - 2)
                    for f in range(FC):
                        act.wait_ge(h_ready, FC * (s - 1) + f + 1)
                        act.activation(hT[:, (q - 1) % 2, f], hidden[(q - 1) % 2 * FC + f], ACT.Gelu,
                                       bias=now1[:, (q - 1) % 3, F + f:F + f + 1]).then_inc(gelu_done, 1)

            run_tiles(act, layers)

            for c in range(NCH):
                act.wait_ge(got_in[c % 2], 32 * (c // 2 + 1))
                after(act, moe, 5 * (c - 1) + 1)
                for i in range(CH):
                    last = act.activation(first[:, i], got[:, c % 2, 0, i], ACT.Copy, scale=wgt[:, CH * c + i, 0:1])
                last.then_inc(first_done, 1)

        @block.vector
        def _(dve):
            dve.memset(q_stack[:, :, :, :].rearrange("p r h q -> p (r h q)").bitcast(U32), 0).then_inc(consts_p, 1)
            dve.memset(k_stack[SHIFT:P, :], 1.0).then_inc(consts_p, 1)
            dve.memset(ones_bf[:, :], 1.0).then_inc(numbered, 1)
            dve.memset(ones_e[:, :], 1.0).then_inc(numbered, 1)
            dve.memset(seen[:, :], 0.0).then_inc(seen_done, 1)
            for e in range(E):
                dve.memset(expert_no[:, e:e + 1], float(e)).then_inc(numbered, 1)
                dve.memset(region_at[:, e:e + 1], float(e * REGION)).then_inc(numbered, 1)
            dve.wait_ge(weights_in, 96)
            dve.tensor_copy(wqk[:, :, :].rearrange("p w (d h) -> p w d h", d=HD),
                            wqk_raw[:, 0:2 * D].rearrange("p (w h d) -> p w d h", w=2, h=H)).then_inc(consts_v, 1)
            dve.wait_ge(iotas, 4)
            dve.tensor_copy(tile_no[:, :], tile_no_i[:, :]).then_inc(numbered, 1)
            dve.wait_ge(gate_turned, 1)
            dve.tensor_copy(gate_t[:, :], G[:, 0:E]).then_inc(consts_v, 1)

            def body(t, r, lap):
                for u in range(NP):
                    if u == 0 and on(t - 5):
                        dve.wait_ge(rank_ready, t - 4)
                        dve.tensor_tensor(row_of[:, :, :], G[:, 0:TT * E].rearrange("p (i e) -> p i e", i=TT),
                                          region_at[:, None, :].broadcast_to([P, TT, E]), ALU.add).then_inc(rank_read, 1)
                        dve.tensor_tensor(seen[:, :], seen[:, :], both[:, 0], ALU.add).then_inc(row_done, 1)
                        dve.wait_ge(rank_read, t - 4)
                        for i in range(TT):
                            dve.tensor_tensor(row_chosen[:, 2 * i:2 * i + 2], chosen[:, i],
                                              row_of[:, i, None, :].broadcast_to([P, 2, E]), ALU.mult).then_inc(row_done, 1)
                        dve.wait_ge(row_done, (TT + 2) * (t - 5) + TT + 1)
                        dve.tensor_reduce(row_f[:, :], row_chosen[:, :, :], X, ALU.add).then_inc(row_done, 1)
                        dve.tensor_tensor(seen[:, :], seen[:, :], both[:, 1], ALU.add).then_inc(seen_done, 1)
                        wait_apart(dve, row_done, (TT + 2) * (t - 4))
                        q = (r - 5) % 3
                        dve.tensor_copy(row_no[:, q * 2 * TT:(q + 1) * 2 * TT], row_f[:, :]).then_inc(row_ready, 1)
                    if u == 0 and on(t - 4):
                        dve.wait_ge(y_ready, t - 3)
                        for i in range(TT):
                            dve.bn_stats(stats[:, i], y[:, i]).then_inc(stats_done, 1)
                        for i in range(TT):
                            wait_apart(dve, stats_done, (2 * TT) * (t - 4) + TT + i)
                            dve.bn_aggr(moments[:, i], stats[:, i]).then_inc(stats_done, 1)
                        dve.wait_ge(stats_done, 2 * TT * (t - 3))
                        dve.tensor_scalar(var_eps[:, :], moments[:, :, 1], EPS, None, ALU.add).then_inc(var_done, 1)
                    if u < NM // 2 and on(t - 1):
                        for i in (2 * u, 2 * u + 1):
                            half, h0, nh = M_UNITS[i]
                            dve.wait_ge(m_ready, NM * (t - 1) + i + 1)
                            if i == 0:
                                after(dve, shift_made, t - 3)
                            dve.tensor_reduce(row_max[:, (r - 1) % 3, h0:h0 + nh, half],
                                              M[i % 2][:, :].rearrange("p (h k) -> p h k", h=nh), X, ALU.max).then_inc(m_reduced, 1)
                    if u == 1 and on(t - 4):
                        dve.wait_ge(rstd_done, t - 3)
                        for i in range(TT):
                            last = dve.tensor_scalar(yn[:, i], y[:, i], moments[:, i, 0:1], rstd[:, i:i + 1],
                                                     ALU.subtract, ALU.mult)
                        last.then_inc(yn_done, 1)
                    if u == 2 and on(t):
                        dve.wait_ge(h_split, t + 1)
                        after(dve, l_split, t)
                        dve.tensor_tensor(rest[:, :, :], G[:, :].rearrange("p (w q) -> p w q", w=2), part_h[:, :, :],
                                          ALU.subtract).then_inc(rest_left, 1)
                    if u == 2 and on(t - 4):
                        dve.wait_ge(ys_done, t - 3)
                        for i in range(TT):
                            dve.bn_stats(stats2[:, i], ys[:, i]).then_inc(stats2_done, 1)
                        for i in range(TT):
                            wait_apart(dve, stats2_done, (2 * TT) * (t - 4) + TT + i)
                            dve.bn_aggr(moments2[:, i], stats2[:, i]).then_inc(stats2_done, 1)
                        dve.wait_ge(stats2_done, 2 * TT * (t - 3))
                        dve.tensor_scalar(var_eps2[:, :], moments2[:, :, 1], EPS, None, ALU.add).then_inc(var2_done, 1)
                    if u == 4 and on(t - 4):
                        dve.wait_ge(rstd2_done, t - 3)
                        after(dve, scattered[(r - 4) % 3], 16 * 2 * TT * (lap + (r - 4) // 3))
                        after(dve, x2_kept, t - 4)
                        for i in range(TT):
                            last = dve.tensor_scalar(x2[:, (r - 4) % 3, 0, i, 0:D], ys[:, i], moments2[:, i, 0:1], rstd2[:, i:i + 1],
                                                     ALU.subtract, ALU.mult)
                        last.then_inc(x2_done, 1)
                        dve.tensor_copy(x2[:, (r - 4) % 3, :, :, D].bitcast(U32),
                                        place[:, t - 4].rearrange("p i k -> p k i")).then_inc(placed, 1)
                    if u in (4, 5) and on(t - 3):
                        i = u - 4
                        dve.wait_ge(o_turned, 2 * (t - 3) + i + 1)
                        turned = G[:, :].rearrange("p (h c) -> p h c", h=H)
                        dve.reciprocal(inv_sum[:, i], turned[:, :, HD]).then_inc(inverted, 1)
                        dve.wait_ge(inverted, 2 * (t - 3) + i + 1)
                        after(dve, on_turned, t - 3)
                        dve.tensor_tensor(heads[:, i].rearrange("p (h d) -> p h d", h=H), turned[:, :, 0:HD],
                                          inv_sum[:, i, :, None].broadcast_to([P, H, HD]), ALU.mult).then_inc(o_normed, 1)
                    if u == 6 and on(t - 1):
                        dve.wait_ge(m_reduced, NM * t)
                        after(dve, shift_turned, t - 3)
                        b = (r - 1) % 3
                        dve.tensor_scalar(shift[:, b, 0], row_max[:, b], -1.0, None, ALU.mult).then_inc(shift_hi, 1)
                        dve.wait_ge(shift_hi, t)
                        dve.scalar_tensor_tensor(out=shift[:, b, 1], in0=row_max[:, b], scalar=-1.0, in1=shift[:, b, 0],
                                                 op0=ALU.mult, op1=ALU.subtract).then_inc(shift_made, 1)
                    if u == 7 and on(t - 4):
                        dve.wait_ge(gate_ready, t - 3)
                        if on(t - 3):
                            dve.wait_ge(on_copied, t - 2)
                        dve.tensor_copy(logits[:, (r - 4) % 3], G[:, T:T + TT * E].rearrange("p (i e) -> p i e", i=TT)).then_inc(logits_done, 1)
                        wait_apart(dve, logits_done, t - 3)
                        for i in range(TT):
                            dve.max(top_v[:, i], logits[:, (r - 4) % 3, i]).then_inc(top_done, 1)
                        for i in range(TT):
                            wait_apart(dve, top_done, TT * (t - 4) + i + 1)
                            dve.max_index(top_i[:, i], top_v[:, i], logits[:, (r - 4) % 3, i]).then_inc(index_done, 1)
                        dve.wait_ge(index_done, TT * (t - 3))
                        dve.tensor_copy(top_v_all[:, t - 4], top_v[:, :, 0:2]).then_inc(top_kept, 1)
                        dve.tensor_copy(top_i_f[:, :, :], top_i[:, :, 0:2]).then_inc(top_kept, 1)
                        dve.wait_ge(top_kept, 2 * (t - 3))
                        for k in range(2):
                            dve.tensor_tensor(chosen[:, :, k], top_i_f[:, :, k, None].broadcast_to([P, TT, E]),
                                              expert_no[:, None, :].broadcast_to([P, TT, E]), ALU.is_equal).then_inc(chosen_done, 1)
                        dve.wait_ge(chosen_done, 2 * (t - 3))
                        dve.tensor_tensor(both[:, :, :], chosen[:, :, 0], chosen[:, :, 1], ALU.add).then_inc(both_done, 1)
                    if u == 7 and on(t - 3):
                        dve.wait_ge(proj_ready, t - 2)
                        dve.wait_ge(residuals, 2 * (t - 3) + 1)
                        after(dve, yn_done, t - 3)
                        dve.tensor_tensor(y[:, :, :], G[:, 0:T].rearrange("p (i d) -> p i d", i=TT), x_bproj[:, :, :],
                                          ALU.add).then_inc(y_ready, 1)

            run(dve, body)

            dve.wait_ge(top_kept, 2 * B)
            tv = top_v_all[:, :, :, :].rearrange("p b i k -> p (b i) k")
            dve.tensor_tensor(diff[:, :], tv[:, :, 1], tv[:, :, 0], ALU.subtract).then_inc(diff_done, 1)
            dve.wait_ge(exp2_done, 1)
            dve.tensor_scalar(esum[:, :], exp2[:, :], 1.0, None, ALU.add).then_inc(wt, 1)
            dve.wait_ge(wt, 1)
            dve.reciprocal(wgt[:, :, 0], esum[:, :]).then_inc(wt, 1)
            dve.wait_ge(wt, 2)
            dve.tensor_tensor(wgt[:, :, 1], wgt[:, :, 0], exp2[:, :], ALU.mult).then_inc(wt, 1)

            dve.wait_ge(counts_ready, 1)
            dve.tensor_tensor(pad_row[:, :], G[:, 0:E], region_at[:, :], ALU.add).then_inc(pad_rows_done, 1)
            dve.tensor_scalar(rounded[:, :], G[:, 0:E], float(P - 1), None, ALU.add).then_inc(table, 1)
            dve.wait_ge(table, 1)
            dve.tensor_scalar(tiles_i[:, :], rounded[:, :], P.bit_length() - 1, None, ALU.arith_shift_right).then_inc(table, 1)
            wait_apart(dve, table, 2)
            dve.tensor_copy(tiles[:, :], tiles_i[:, :]).then_inc(table, 1)
            dve.wait_ge(table, 3)
            dve.tensor_tensor_scan(tiles_end[:, :], ones_e[:, :], tiles[:, :], 0.0, ALU.mult, ALU.add).then_inc(table, 1)
            dve.tensor_scalar(skip[:, :], tiles[:, :], -float(P), float(REGION), ALU.mult, ALU.add).then_inc(table, 1)
            dve.wait_ge(table, 5)
            dve.tensor_scalar(ended[:, :], tiles_end[:, :], tile_no[:, 0:1], None, ALU.is_le).then_inc(table, 1)
            dve.wait_ge(table, 6)
            dve.tensor_tensor(skipped[:, :], ended[:, :], skip[:, :], ALU.mult).then_inc(table, 1)
            dve.tensor_reduce(n_ended[:, :], ended[:, :], X, ALU.add).then_inc(table, 1)
            dve.wait_ge(table, 8)
            dve.tensor_reduce(n_skipped[:, :], skipped[:, :], X, ALU.add).then_inc(table, 1)
            dve.tensor_scalar(tile_f[:, 0:1], n_ended[:, :], float(E - 1), None, ALU.min).then_inc(tile_f_done, 1)
            dve.wait_ge(table, 9)
            dve.scalar_tensor_tensor(out=tile_f[:, 1:2], in0=tile_no[:, :], scalar=float(P), in1=n_skipped[:, :],
                                     op0=ALU.mult, op1=ALU.add).then_inc(tile_f_done, 1)
            dve.wait_ge(tile_turned, 1)
            dve.tensor_scalar(tile_i[:, :, :], G[0:1, 0:2 * P].rearrange("p (w t) -> p w t", w=2), float(E * REGION), None,
                              ALU.min).then_inc(tile_i_done, 1)
            dve.wait_ge(tile_i_done, 1)
            dve.wait_ge(experts_in, 80)

            def layers(s, q, turn):
                if is_tile(s):
                    e = dve.value_load(tile_i[0:1, 0, bass.ds(s, 1)], min_val=0, max_val=E - 1)
                    after(dve, gelu_done, FC * (s - 2))
                    dve.tensor_copy(now1[:, q % 3], layer1[:, bass.ds(e * (F + FC), F + FC)]).then_inc(layer_now, 1)
                if is_tile(s - 2):
                    e = dve.value_load(tile_i[0:1, 0, bass.ds(s - 2, 1)], min_val=0, max_val=E - 1)
                    dve.wait_ge(layer2_done, s - 1)
                    before = turn - (1 if q < 2 else 0)
                    after(dve, sent[(q - 2) % XR], 16 * before)
                    dve.tensor_tensor(y_rows[:, (q - 2) % XR], M[q % 2][:, 0:D], bias2[:, bass.ds(e * D, D)],
                                      ALU.add).then_inc(y_biased, 1)

            run_tiles(dve, layers)

            for c in range(NCH):
                dve.wait_ge(first_done, c + 1)
                x2c = x2_all[:, 2 * c:2 * c + 2, :].rearrange("p b (i d) -> p (b i) d", d=D)
                for i in range(CH):
                    last = dve.scalar_tensor_tensor(out=acc[:, i], in0=got[:, c % 2, 1, i], scalar=wgt[:, CH * c + i, 1:2],
                                                    in1=first[:, i], op0=ALU.mult, op1=ALU.add)
                last.then_inc(moe, 1)
                dve.wait_ge(moe, 5 * c + 1)
                dve.tensor_tensor(summed[:, :, :], acc[:, :, :], x2c, ALU.add).then_inc(moe, 1)
                dve.wait_ge(moe, 5 * c + 2)
                dve.tensor_scalar(clipped[:, :, :], summed[:, :, :], 100.0, -100.0, ALU.min, ALU.max).then_inc(moe, 1)
                dve.wait_ge(moe, 5 * c + 3)
                dve.tensor_tensor(x3[:, :, :], clipped[:, :, :], x2c, ALU.add).then_inc(moe, 1)
                dve.wait_ge(moe, 5 * c + 4)
                for i in range(CH):
                    last = dve.bn_stats(stats3[:, i], x3[:, i])
                last.then_inc(moe, 1)
                dve.wait_ge(moe, 5 * c + 5)
                for i in range(CH):
                    last = dve.bn_aggr(moments3[:, i], stats3[:, i])
                last.then_inc(moe_aggr, 1)
                dve.wait_ge(moe_aggr, c + 1)
                dve.tensor_scalar(var_eps3[:, :], moments3[:, :, 1], EPS, None, ALU.add).then_inc(moe_var, 1)
                dve.wait_ge(moe_rstd, c + 1)
                after(dve, out_sent, 16 * c)
                for i in range(CH):
                    last = dve.tensor_scalar(fin[:, i], x3[:, i], moments3[:, i, 0:1], rstd3[:, i:i + 1],
                                             ALU.subtract, ALU.mult)
                last.then_inc(fin_done, 1)

        @block.tensor
        def _(pe):
            pe.wait_ge(consts, 8)
            pe.wait_ge(weights_in, 96)
            pe.transpose(G[:, 0:E], gate_raw[:, :], ident[0:E, 0:E]).then_inc(gate_turned, 1)
            pe.wait_ge(consts_v, 2)

            def scores(t, r, s, n):
                after(pe, exp_done, NP * s + n - 1)
                if n == 0:
                    pe.wait_ge(shifted, 16 * (s + 1))
                b = (r - (2 if n < NP - 2 else 3)) % 3
                for j in range(2):
                    h = 2 * n + j
                    pe.matmul(S[n % 2][:, j * T:j * T + T], k_stack[:, b, h, 0:P], q_stack[:, b, h, :],
                              start=True, stop=True)
                for j in range(2):
                    h = 2 * n + j
                    last = pe.matmul(S[n % 2][:, 2 * T + j * P:2 * T + j * P + P], k_stack[:, b, h, P:T],
                                     q_stack[:, b, h, P:T], start=True, stop=True)
                last.then_inc(s_ready, 1)

            def maxima(t, r, i):
                half, h0, nh = M_UNITS[i]
                keys = P * (half + 1)
                if i == 0:
                    pe.wait_ge(stacked, 16 * 12 * t)
                after(pe, m_reduced, NM * (t - 1) + i - 1)
                b = (r - 1) % 3
                bank = M[i % 2]
                for j in range(nh):
                    pe.matmul(bank[:, j * keys:j * keys + keys], q_stack[0:SHIFT, b, h0 + j, half * P:half * P + P],
                              k_stack[0:SHIFT, b, h0 + j, 0:keys], start=(j == 0), stop=False, skip_group_check=True)
                diag = bank[:, :].rearrange("p (h k) -> p h k", h=nh)[:, :, keys - P:keys]
                pe.matmul(diag, ident_bf[:, :], causal_neg[:, None, :].broadcast_to([P, nh, P]), start=False, stop=True,
                          skip_group_check=True).then_inc(m_ready, 1)

            def values(t, r, s, k):
                pe.wait_ge(masked, NP * s + 2 * k + 2)
                if k == 0:
                    pe.wait_ge(v_copied, s + 1)
                if k % 2 == 0:
                    after(pe, o_copied, 2 * s + k // 2)
                b = (r - (2 if k < 2 else 3)) % 3
                at = (k % 2) * T
                for j in range(4):
                    h = 4 * k + j
                    pe.matmul(O[32 * j:32 * j + 32, at:at + T], v_aug[:, b, 0, h], probs[:, h // 2, (h % 2) * T:(h % 2) * T + T],
                              start=True, stop=False, skip_group_check=True)
                for j in range(4):
                    h = 4 * k + j
                    last = pe.matmul(O[32 * j:32 * j + 32, at + P:at + T], v_aug[:, b, 1, h],
                                     probs[:, h // 2, 2 * T + (h % 2) * P:2 * T + (h % 2) * P + P],
                                     start=False, stop=True, skip_group_check=True)
                last.then_inc(pv_done, 1)

            def body(t, r, lap):
                for u in range(NP):
                    s, n = s_unit(t, u)
                    if on(s):
                        scores(t, r, s, n)
                    if u == 0 and on(t - 5):
                        pe.wait_ge(both_done, t - 4)
                        pe.wait_ge(seen_done, t - 4)
                        if on(t - 4):
                            pe.wait_ge(y_ready, t - 3)
                        for i in range(TT):
                            rank = G[:, i * E:i * E + E]
                            pe.matmul(rank, earlier[:, :], both[:, i], start=True, stop=False, skip_group_check=True)
                            for j in range(i):
                                pe.matmul(rank, ones_bf[:, :], both[:, j], start=False, stop=False, skip_group_check=True)
                            last = pe.matmul(rank, ones_bf[:, :], seen[:, :], start=False, stop=True, skip_group_check=True)
                        last.then_inc(rank_ready, 1)
                    if u == 1 and on(t - 5):
                        pe.wait_ge(rank_read, t - 4)
                    if u == 1 and on(t):
                        if on(t - 4):
                            pe.wait_ge(y_ready, t - 3)
                        elif on(t - 2):
                            pe.wait_ge(shift_copied, t - 1)
                        elif on(t - 1):
                            pe.wait_ge(v_copied, t)
                        pe.wait_ge(x_in[r], 16 * (lap + 1))
                        for i in range(TT):
                            last = pe.transpose(G[:, i * P:i * P + P], xin[:, r, i], ident[:, :])
                        last.then_inc(xT_ready, 1)
                    if u == 2 and on(t):
                        pe.wait_ge(xT_copied, t + 1)
                        for w in range(2):
                            last = pe.matmul(G[:, w * T:w * T + T], wqk[:, w], xT[:, r], start=True, stop=True)
                        last.then_inc(qk_ready, 1)
                    if u == 3 and on(t):
                        pe.wait_ge(h_split, t + 1)
                        pe.wait_ge(rest_left, t + 1)
                        for i in range(TT):
                            last = pe.matmul(G[:, i * P:i * P + P], xT[:, r, i * P:i * P + P], wqk_raw[:, 2 * D:3 * D],
                                             start=True, stop=True)
                        last.then_inc(v_ready, 1)
                    if u < NM // 2 and on(t - 1):
                        maxima(t, r, 2 * u)
                        maxima(t, r, 2 * u + 1)
                    if pv_quad(t, u) and on(pv_quad(t, u)[0]):
                        values(t, r, *pv_quad(t, u))
                    if u in (4, 5) and on(t - 3):
                        i = u - 4
                        pe.wait_ge(o_copied, 2 * (t - 2))
                        if on(t):
                            pe.wait_ge(v_copied, t + 1)
                        elif i == 0 and on(t - 4):
                            pe.wait_ge(y_ready, t - 3)
                        after(pe, o_normed, 2 * (t - 3) + i)
                        for k in range(4):
                            last = pe.transpose(G[:, k * P:k * P + P], heads_t[:, k, i * P:i * P + P], ident[:, :])
                        last.then_inc(o_turned, 1)
                    if u == 5 and on(t - 4):
                        pe.wait_ge(x2_done, t - 3)
                        if on(t - 3):
                            pe.wait_ge(o_normed, 2 * (t - 2))
                        else:
                            pe.wait_ge(y_ready, t - 3)
                        for i in range(TT):
                            last = pe.transpose(G[:, i * P:i * P + P], x2[:, (r - 4) % 3, 0, i, 0:D], ident[:, :])
                        last.then_inc(x2T_ready, 1)
                    if u == 6 and on(t - 4):
                        pe.wait_ge(x2T_copied, t - 3)
                        for i in range(TT):
                            last = pe.matmul(G[:, T + i * E:T + i * E + E], x2T[:, (r - 4) % 3, i * P:i * P + P], gate_t[:, :],
                                             start=True, stop=True)
                        last.then_inc(gate_ready, 1)
                    if u == 6 and on(t - 3):
                        pe.wait_ge(o_normed, 2 * (t - 2))
                        for i in range(TT):
                            last = pe.transpose(G[:, i * P:i * P + P], heads[:, i], ident[:, :])
                        last.then_inc(on_turned, 1)
                    if u == 7 and on(t - 1):
                        wait_apart(pe, shift_made, t)
                        if on(t - 4):
                            pe.wait_ge(logits_done, t - 3)
                        if on(t - 3):
                            pe.wait_ge(on_copied, t - 2)
                        elif on(t):
                            pe.wait_ge(v_copied, t + 1)
                        pe.transpose(G_bf[0:2 * H * TT, 0:P], shift[:, (r - 1) % 3].rearrange("p w h i -> p (w h i)"),
                                     ident_bf[:, :]).then_inc(shift_turned, 1)
                    if u == 7 and on(t - 3):
                        pe.wait_ge(on_copied, t - 2)
                        if on(t - 4):
                            pe.wait_ge(logits_done, t - 3)
                        if on(t - 1):
                            pe.wait_ge(shift_copied, t)
                        for i in range(TT):
                            last = pe.matmul(G[:, i * P:i * P + P], heads_n_t[:, i * P:i * P + P], wproj[:, :],
                                             start=True, stop=True)
                        last.then_inc(proj_ready, 1)

            run(pe, body)

            pe.wait_ge(seen_done, B + 1)
            pe.wait_ge(rank_read, B)
            pe.matmul(G[:, 0:E], ones_bf[:, :], seen[:, :], start=True, stop=True).then_inc(counts_ready, 1)
            pe.wait_ge(tile_f_done, 2)
            for w in range(2):
                last = pe.transpose(G[0:1, w * P:w * P + P], tile_f[:, w:w + 1], ident[:, :])
            last.then_inc(tile_turned, 1)
            pe.wait_ge(tile_i_done, 1)
            pe.wait_ge(experts_in, 80)
            pe.wait_ge(o_copied, 2 * B)
            pe.wait_ge(exp_done, NP * B)
            pe.wait_ge(m_reduced, NM * B)

            def layers(s, q, turn):
                if is_tile(s):
                    pe.wait_ge(rows_in[q], 16 * (turn + 1))
                    after(pe, rows_copied, s - 1)
                    pe.transpose((G, O)[q % 2][:, 0:P], rows[:, q, 0:D], ident[:, :]).then_inc(rows_turned, 1)
                if is_tile(s - 1):
                    pe.wait_ge(rows_copied, s)
                    pe.wait_ge(layer_now, s)
                    after(pe, gelu_done, FC * (s - 2))
                    for f in range(FC):
                        pe.matmul(hidden[(q - 1) % 2 * FC + f], now1[:, (q - 1) % 3, f * P:f * P + P], rows_t[:, (q - 1) % 2],
                                  start=True, stop=True).then_inc(h_ready, 1)
                if is_tile(s - 2):
                    e = pe.value_load(tile_i[0:1, 0, bass.ds(s - 2, 1)], min_val=0, max_val=E - 1)
                    pe.wait_ge(gelu_done, FC * (s - 1))
                    after(pe, y_biased, s - 3)
                    for f in range(FC):
                        last = pe.matmul(M[q % 2][:, 0:D], hT[:, q % 2, f], layer2[:, bass.ds(e * F + f * P, D)],
                                         start=(f == 0), stop=(f == FC - 1))
                    last.then_inc(layer2_done, 1)

            run_tiles(pe, layers)


_INS = ['L0_attn_target', 'L0_attn_w_qkv', 'L0_attn_w_proj', 'L0_attn_b_proj', 'L0_attn_ln_gamma', 'L0_attn_ln_beta',
        'L0_ffn_gate_w', 'L0_ffn_w1', 'L0_ffn_b1', 'L0_ffn_w2', 'L0_ffn_b2']
_OUTS = [((16, 256, 128), 'float32')]


def kernel(**inputs):
    import numpy as _np
    import concourse.bacc as _bacc
    from concourse import mybir as _mybir
    from concourse.bass_utils import run_bass_kernel_spmd as _run

    nc = _bacc.Bacc("TRN2", target_bir_lowering=False, num_devices=1)
    arrays, args = {}, []
    for name in _INS:
        a = _np.ascontiguousarray(inputs[name])
        arrays[f"in_{name}_dram"] = a
        args.append(nc.dram_tensor(f"in_{name}_dram", a.shape, _mybir.dt.from_np(a.dtype), kind="ExternalInput").ap())
    for i, (shape, dtype) in enumerate(_OUTS):
        dt = _mybir.dt.from_np(_np.dtype(dtype))
        args.append(nc.dram_tensor(f"out_{i}_dram", shape, dt, kind="ExternalOutput").ap())
    transformer_layer(nc, *args)
    r = _run(nc, [arrays], core_ids=[0])
    got = tuple(r.results[0][f"out_{i}_dram"] for i in range(len(_OUTS)))
    return got[0]
```

```python
from contextlib import ExitStack

import concourse.bass as bass
from concourse import mybir

F32 = mybir.dt.float32
BF16 = mybir.dt.bfloat16
U32 = mybir.dt.uint32
I32 = mybir.dt.int32
ALU = mybir.AluOpType
ACT = mybir.ActivationFunctionType
X = mybir.AxisListType.X

P = 128
H = 16
EPS = 1e-5
NEG = -1e30


def after(eng, sem, count):
    if not isinstance(count, int) or count > 0:
        eng.wait_ge(sem, count)


def transformer_layer(nc, x, w_qkv, w_proj, b_proj, ln_gamma, ln_beta, gate_w, w1, b1, w2, b2, out):
    B, T, D = x.shape
    E, _, F = w1.shape
    HD = D // H
    SCALE = float(HD) ** -0.5
    TT = T // P
    NT = B * TT
    FC = F // P
    NP = H // 2
    SHIFT = 96
    assert D == P and T == 2 * P and H * HD == P
    N = B * T
    REGION = N + P
    ROW = D + 1
    XR = 6
    TILES = -(-(2 * N // P + E - 1) // XR) * XR
    PADS = TT + 1
    EXPERT_BITS = 4
    BLOCK_BITS = 10
    assert E <= 1 << EXPERT_BITS and EXPERT_BITS * XR <= 24
    assert TILES // XR % 2 == 1
    assert REGION % P == 0 and E * (REGION // P) < 1 << BLOCK_BITS and XR % 2 == 0

    def on(s):
        return not isinstance(s, int) or 0 <= s < B

    def early(t):
        return isinstance(t, int) and t < 4

    def is_tile(s):
        return not isinstance(s, int) or 0 <= s < TILES

    sorted_rows = nc.dram_tensor("sorted_rows", (E * REGION + P, ROW), F32, kind="Internal").ap()
    results = nc.dram_tensor("results", (2 * N, D), F32, kind="Internal").ap()

    x_tiles = x.rearrange("b (i p) d -> b p i d", p=P)
    out_chunks = out.rearrange("(c b) (i p) d -> c p (b i) d", b=2, p=P)

    with ExitStack() as ctx:
        def sb(name, shape, dt=F32):
            return ctx.enter_context(nc.sbuf_tensor(name, shape, dt))

        def ps(name, shape, dt=F32):
            return ctx.enter_context(nc.psum_tensor(name, shape, dt))

        def sem(name):
            return ctx.enter_context(nc.semaphore(name))

        ident = sb("ident", [P, P])
        ident_bf = sb("ident_bf", [P, P], BF16)
        causal_neg = sb("causal_neg", [P, P], BF16)
        minus_half = sb("minus_half", [P, 4])
        warm = sb("warm", [P, 1])
        expert_no = sb("expert_no", [P, E])
        wqk_raw = sb("wqk_raw", [P, 3 * D])
        wqk = sb("wqk", [P, 2, D])
        wproj = sb("wproj", [P, D])
        gate_raw = sb("gate_raw", [E, D])
        gate_t = sb("gate_t", [P, E])
        bproj_all = sb("bproj_all", [P, D])
        gamma_all = sb("gamma_all", [P, D])
        beta_all = sb("beta_all", [P, D])
        AT_B1, AT_B2, AT_W2, SIZE = F, F + FC, F + FC + D, F + FC + D + F
        experts = sb("experts", [P, E * SIZE])
        earlier = sb("earlier", [P, P], BF16)
        ones_bf = sb("ones_bf", [P, P], BF16)
        region_at = sb("region_at", [P, E])
        tile_no = sb("tile_no", [P, 1])
        tile_no_i = sb("tile_no_i", [P, 1], I32)
        place = sb("place", [P, B, TT, 2], U32)
        pad = sb("pad", [P, PADS, ROW])
        expert_unit = sb("expert_unit", [1, XR])
        block_unit = sb("block_unit", [1, 2])
        xin = sb("xin", [P, 3, TT, D])
        xres = sb("xres", [P, 3, TT, D])
        xT = sb("xT", [P, 3, T])
        part_h = sb("part_h", [P, 3, 2, T], BF16)
        part_m = sb("part_m", [P, 3, 2, T], BF16)
        part_l = sb("part_l", [P, 3, 2, T], BF16)
        rest = sb("rest", [P, 2, T])
        v_aug = sb("v_aug", [P, 3, TT, H, 32])
        q_stack = sb("q_stack", [P, 3, H, T], BF16)
        k_stack = sb("k_stack", [P, 3, H, T], BF16)
        row_max = sb("row_max", [P, 3, H, TT])
        shift = sb("shift", [P, 3, 2, H, TT], BF16)
        shift_t = sb("shift_t", [2 * H * TT, 3, P], BF16)
        probs = sb("probs", [P, NP, 3 * T])
        heads_t = sb("heads_t", [P, 4, T])
        inv_sum = sb("inv_sum", [P, TT, H])
        heads = sb("heads", [P, TT, D])
        heads_n_t = sb("heads_n_t", [P, T])
        x_bproj = sb("x_bproj", [P, TT, D])
        x_beta = sb("x_beta", [P, TT, D])
        y = sb("y", [P, TT, D])
        stats = sb("stats", [P, TT, 6])
        moments = sb("moments", [P, TT, 2])
        neg_mean = sb("neg_mean", [P, TT])
        neg_mean2 = sb("neg_mean2", [P, TT])
        centre1 = sb("centre1", [P, TT])
        centre2 = sb("centre2", [P, TT])
        var_eps = sb("var_eps", [P, TT])
        rstd = sb("rstd", [P, TT])
        yn = sb("yn", [P, TT, D])
        yg = sb("yg", [P, TT, D])
        ys = sb("ys", [P, TT, D])
        stats2 = sb("stats2", [P, TT, 6])
        moments2 = sb("moments2", [P, TT, 2])
        var_eps2 = sb("var_eps2", [P, TT])
        rstd2 = sb("rstd2", [P, TT])
        x2 = sb("x2", [P, 3, 2, TT, ROW])
        x2_all = sb("x2_all", [P, B, TT * D])
        x2T = sb("x2T", [P, 3, T])
        logits = sb("logits", [P, 3, TT, E])
        top_v = sb("top_v", [P, TT, 8])
        top_i = sb("top_i", [P, TT, 8], U32)
        top_v_all = sb("top_v_all", [P, B, TT, 2])
        top_i_f = sb("top_i_f", [P, TT, 2])
        chosen = sb("chosen", [P, TT, 2, E])
        both = sb("both", [P, TT, E], BF16)
        seen = sb("seen", [P, E], BF16)
        row_of = sb("row_of", [P, TT, E])
        row_chosen = sb("row_chosen", [P, TT * 2, E])
        row_f = sb("row_f", [P, TT * 2])
        row_no = sb("row_no", [P, 3 * TT * 2], U32)
        pad_row = sb("pad_row", [P, E], I32)
        rounded = sb("rounded", [P, E], I32)
        tiles_i = sb("tiles_i", [P, E], I32)
        tiles = sb("tiles", [P, E])
        ones_e = sb("ones_e", [P, E])
        tiles_end = sb("tiles_end", [P, E])
        ended = sb("ended", [P, E])
        skip = sb("skip", [P, E])
        skipped = sb("skipped", [P, E])
        n_ended = sb("n_ended", [P, 1])
        n_skipped = sb("n_skipped", [P, 1])
        tile_f = sb("tile_f", [P, 2])
        expert_part = sb("expert_part", [1, TILES])
        block_part = sb("block_part", [1, TILES])
        expert_sum = sb("expert_sum", [1, TILES // XR])
        block_sum = sb("block_sum", [1, TILES // 2])
        expert_word = sb("expert_word", [1, TILES // XR], I32)
        block_word = sb("block_word", [1, TILES // 2], I32)

        CH = 2 * TT
        NCH = NT // CH
        diff = sb("diff", [P, NT])
        exp2 = sb("exp2", [P, NT])
        esum = sb("esum", [P, NT])
        wgt = sb("wgt", [P, NT, 2])
        rows = sb("rows", [P, XR, ROW])
        rows_t = sb("rows_t", [P, 2, P])
        expert_now = probs[:, :, :].rearrange("p n q -> p (n q)")[:, 0:XR * SIZE].rearrange("p (s n) -> p s n", s=XR)
        hT = sb("hT", [P, 2, FC, P])
        y_rows = sb("y_rows", [P, XR, ROW])
        got = [stack[:, :, :, :].rearrange("p r h q -> p (r h q)").bitcast(F32)[:, 0:NT * D].rearrange(
            "p (i d) -> p i d", d=D) for stack in (q_stack, k_stack)]
        late = probs[:, :, :].rearrange("p n q -> p (n q)")
        moe, acc = (late[:, n * CH * D:(n + 1) * CH * D].rearrange("p (i d) -> p i d", d=D) for n in range(2))
        first, second, clipped, fin = (late[:, (2 + 2 * n) * CH * D:(4 + 2 * n) * CH * D].rearrange("p (c i d) -> p c i d", c=2, d=D)
                             for n in range(4))
        minus_mean = sb("minus_mean", [P, 2, CH])
        stats3 = sb("stats3", [P, CH, 6])
        moments3 = sb("moments3", [P, CH, 2])
        var_eps3 = sb("var_eps3", [P, CH])
        rstd3 = sb("rstd3", [P, 2, CH])

        S = [ps(f"S{i}", [P, 1024]) for i in range(2)]
        M = [ps(f"M{i}", [P, 512]) for i in range(2)]
        O = ps("O", [P, 512])
        G = ps("G", [P, 512])
        M1_bf = M[1][:, :].bitcast(BF16)
        hidden = [S[i // FC][:, (i % FC) * 512:(i % FC) * 512 + P] for i in range(2 * FC)]

        weights_in = sem("weights_in")
        experts_in = sem("experts_in")
        consts = sem("consts")
        consts_v = sem("consts_v")
        warmed = sem("warmed")
        consts_p = sem("consts_p")
        stack_ones = sem("stack_ones")
        keys_zeroed = [sem(f"keys_zeroed{i}") for i in range(3)]
        queries_zeroed = [sem(f"queries_zeroed{i}") for i in range(3)]
        gate_turned = sem("gate_turned")
        x_in = [sem(f"x_in{i}") for i in range(3)]
        xres_in = [sem(f"xres_in{i}") for i in range(3)]
        stacked = [sem(f"stacked{i}") for i in range(3)]
        shifted = sem("shifted")
        xT_ready = sem("xT_ready")
        xT_copied = sem("xT_copied")
        qk_ready = sem("qk_ready")
        h_split = sem("h_split")
        rest_left = sem("rest_left")
        m_split = sem("m_split")
        l_split = sem("l_split")
        v_ready = sem("v_ready")
        v_copied = sem("v_copied")
        m_ready = sem("m_ready")
        m_reduced = sem("m_reduced")
        shift_hi = sem("shift_hi")
        shift_made = sem("shift_made")
        shift_turned = sem("shift_turned")
        shift_copied = sem("shift_copied")
        s_ready = sem("s_ready")
        exp_done = sem("exp_done")
        masked = sem("masked")
        pv_done = sem("pv_done")
        o_copied = sem("o_copied")
        o_turned = sem("o_turned")
        inverted = sem("inverted")
        o_normed = sem("o_normed")
        on_turned = sem("on_turned")
        on_copied = sem("on_copied")
        proj_ready = sem("proj_ready")
        residuals = sem("residuals")
        y_ready = sem("y_ready")
        stats_done = sem("stats_done")
        var_done = sem("var_done")
        centred = sem("centred")
        centred2 = sem("centred2")
        rstd_done = sem("rstd_done")
        yn_done = sem("yn_done")
        yg_done = sem("yg_done")
        ys_done = sem("ys_done")
        stats2_done = sem("stats2_done")
        var2_done = sem("var2_done")
        rstd2_done = sem("rstd2_done")
        x2_done = sem("x2_done")
        x2_kept = sem("x2_kept")
        x2T_ready = sem("x2T_ready")
        x2T_copied = sem("x2T_copied")
        x2_twice = sem("x2_twice")
        placed = sem("placed")
        gate_ready = sem("gate_ready")
        logits_done = sem("logits_done")
        top_done = sem("top_done")
        index_done = sem("index_done")
        top_kept = sem("top_kept")
        numbered = sem("numbered")
        iotas = sem("iotas")
        chosen_done = sem("chosen_done")
        both_done = sem("both_done")
        seen_done = sem("seen_done")
        rank_ready = sem("rank_ready")
        rank_read = sem("rank_read")
        row_done = sem("row_done")
        row_ready = sem("row_ready")
        scattered = [sem(f"scattered{i}") for i in range(3)]
        counts_ready = sem("counts_ready")
        table = sem("table")
        pad_rows_done = sem("pad_rows_done")
        tile_f_done = sem("tile_f_done")
        tile_turned = sem("tile_turned")
        tile_parts = sem("tile_parts")
        tile_sums = sem("tile_sums")
        words_done = sem("words_done")
        padded = sem("padded")
        rows_in = [sem(f"rows_in{i}") for i in range(XR)]
        sent = [sem(f"sent{i}") for i in range(XR)]
        rows_turned = sem("rows_turned")
        rows_copied = sem("rows_copied")
        expert_ready = sem("expert_ready")
        got_in = [sem(f"got_in{i}") for i in range(2)]
        second_done = sem("second_done")
        moe_done = sem("moe_done")
        first_done = sem("first_done")
        minus_mean_done = sem("minus_mean_done")
        acc_done = sem("acc_done")
        clipped_done = sem("clipped_done")
        x3_done = sem("x3_done")
        stats3_done = sem("stats3_done")
        ids_copied = sem("ids_copied")
        diff_done = sem("diff_done")
        exp2_done = sem("exp2_done")
        wt = sem("wt")
        h_ready = sem("h_ready")
        gelu_done = sem("gelu_done")
        y_biased = sem("y_biased")
        layer2_done = sem("layer2_done")
        moe_aggr = sem("moe_aggr")
        moe_var = sem("moe_var")
        moe_rstd = sem("moe_rstd")
        fin_done = sem("fin_done")
        out_sent = [sem(f"out_sent{i}") for i in range(2)]

        FIRST, LAST = 7, 7 + (B - 1 - 7) // 3 * 3

        def run(eng, body):
            for t in range(FIRST):
                body(t, t % 3, t // 3)
            with eng.Fori(0, (LAST - FIRST) // 3) as i:
                for k in range(3):
                    body(i * 3 + (FIRST + k), (FIRST + k) % 3, i + (FIRST + k) // 3)
            for t in range(LAST, B + 5):
                body(t, t % 3, t // 3)

        def run_tiles(eng, body):
            for s in range(XR):
                body(s, s % XR, s // XR)
            with eng.Fori(0, (TILES // XR - 1) // 2) as i:
                for k in range(2 * XR):
                    body(i * (2 * XR) + (XR + k), k % XR, i * 2 + (1 + k // XR))
            for s in range(TILES, TILES + 3):
                body(s, s % XR, s // XR)

        def x3(c, i):
            return x2_all[:, 2 * c + i // TT, (i % TT) * D:(i % TT) * D + D]

        def run_chunks(eng, *stages):
            def body(c, half):
                for lag, stage in stages:
                    if 0 <= c - lag < NCH:
                        stage(c - lag, (half - lag) % 2)

            for c in range(NCH + 4):
                body(c, c % 2)

        M_UNITS = []
        for p in range(NP):
            M_UNITS.append((1, 2 * p, 2))
            if p % 2:
                M_UNITS.append((0, 2 * p - 2, 4))
        NM = len(M_UNITS)

        def m_units(u):
            return range(max(0, 2 * u - 1), min(NM, 2 * u + 1))

        def s_unit(t, u):
            return (t - 2, u - 2) if u >= 2 else (t - 3, u + NP - 2)

        def pv_quad(t, u):
            return {2: (t - 3, 2), 3: (t - 3, 3), 5: (t - 2, 0), 7: (t - 2, 1)}.get(u)

        def wait_apart(eng, sem, count, *more):
            if not isinstance(count, int):
                count = eng.to_reg(count)
            elif count <= 0:
                return
            eng.wait_ge(weights_in, 96)
            for s in (sem, *more):
                eng.wait_ge(s, count)

        def zeroed(stack):
            return stack.rearrange("p h q -> p (h q)").bitcast(U32)

        ACT_PADS = E // 4

        def pad_experts(eng, some):
            for e in some:
                at = eng.value_load(pad_row[0:1, e:e + 1], min_val=0, max_val=E * REGION - PADS * P)
                eng.dma_start(sorted_rows[bass.ds(at, PADS * P)].rearrange("(p j) d -> p j d", j=PADS),
                              pad[:, :, :]).then_inc(padded, 16)

        def experts_of(eng, turn):
            return eng.value_load(expert_word[0:1, bass.ds(turn, 1)], min_val=0, max_val=(1 << EXPERT_BITS * XR) - 1)

        def expert(word, q):
            return ((word >> EXPERT_BITS * q) & ((1 << EXPERT_BITS) - 1)).with_bounds(min_val=0, max_val=E - 1)

        block = ctx.enter_context(nc.Block())

        @block.sync
        def _(sp):
            sp.dma_start(xin[:, 0], x_tiles[0]).then_inc(x_in[0], 16)
            sp.dma_start(wqk_raw[:, :], w_qkv).then_inc(weights_in, 16)
            sp.dma_start(gate_raw[:, :], gate_w).then_inc(weights_in, 16)
            sp.dma_start(wproj[:, :], w_proj).then_inc(weights_in, 16)
            for to, row in ((bproj_all, b_proj), (gamma_all, ln_gamma), (beta_all, ln_beta)):
                sp.dma_start(to[:, :], row.rearrange("(o d) -> o d", o=1).broadcast_to([P, D])).then_inc(weights_in, 16)

            def load_experts(t):
                by_expert = experts[:, :].rearrange("p (e n) -> p e n", e=E)
                w2_parts = [(by_expert[:, :, AT_W2 + c * D:AT_W2 + c * D + D], w2[:, c * P:c * P + P].rearrange("e f d -> f e d"))
                            for c in range(FC)]
                b1_parts = [(by_expert[:, :, AT_B1 + c], b1[:, c * P:c * P + P].rearrange("e f -> f e")) for c in range(FC)]
                b2_part = (by_expert[:, :, AT_B2:AT_W2], b2.rearrange("(o e) d -> o e d", o=1).broadcast_to([P, E, D]))
                w1_part = (by_expert[:, :, 0:F], w1.rearrange("e d f -> d e f"))
                with nc.allow_non_contiguous_dma(reason="small"):
                    for to, part in {1: [w1_part], 2: w2_parts, 3: [b2_part, *b1_parts]}[t]:
                        sp.dma_start(to, part).then_inc(experts_in, 16)

            def body(t, r, lap):
                if on(t + 1):
                    after(sp, xT_ready, t - 1)
                    sp.dma_start(xin[:, (r + 1) % 3], x_tiles[t + 1]).then_inc(x_in[(r + 1) % 3], 16)
                if on(t - 2):
                    after(sp, residuals, 2 * (t - 4))
                    sp.dma_start(xres[:, (r - 2) % 3], x_tiles[t - 2]).then_inc(xres_in[(r - 2) % 3], 16)
                if on(t):
                    stepped = t + 1 if isinstance(t, int) else sp.to_reg(t + 1)
                    after(sp, s_ready, NP * (t - 2))
                    for done, parts in (
                        (h_split, ((q_stack, part_h, 0, (0, 1, 3)), (k_stack, part_h, 1, (0, 2, 4)))),
                        (m_split, ((q_stack, part_m, 0, (2, 5)), (k_stack, part_m, 1, (1, 5)))),
                        (l_split, ((q_stack, part_l, 0, (4,)), (k_stack, part_l, 1, (3,)))),
                    ):
                        sp.wait_ge(done, stepped)
                        if done is h_split and isinstance(t, int) and t < 3:
                            sp.wait_ge(queries_zeroed[t], 1)
                            sp.wait_ge(keys_zeroed[t], 1)
                        for stack, part, which, places in parts:
                            for n in places:
                                sp.dma_start(stack[HD * n:HD * n + HD, r], part[:, r, which]).then_inc(stacked[r], 16)
                if on(t - 1):
                    sp.wait_ge(shift_copied, t)
                    sp.dma_start(q_stack[SHIFT:SHIFT + 2, (r - 1) % 3], shift_t[:, (r - 1) % 3]).then_inc(shifted, 16)
                if isinstance(t, int) and 1 <= t <= 3:
                    load_experts(t)
                if isinstance(t, int) and t == B + 3:
                    sp.wait_ge(iotas, 6)
                    sp.dma_start(sorted_rows[bass.ds(E * REGION, P)], pad[:, 0]).then_inc(padded, 16)
                    sp.wait_ge(pad_rows_done, 1)
                    pad_experts(sp, range(2 * ACT_PADS, E))

            run(sp, body)

            for i in range(3):
                sp.wait_ge(scattered[i], 16 * 2 * TT * len(range(i, B, 3)))
            sp.wait_ge(words_done, 2)
            blocks = [0]

            def load_rows(s, q, turn):
                if is_tile(s):
                    if q % 2 == 0:
                        blocks[0] = sp.value_load(block_word[0:1, bass.ds(turn * (XR // 2) + q // 2, 1)], min_val=0,
                                                  max_val=(1 << 2 * BLOCK_BITS) - 1)
                    n = (blocks[0] >> BLOCK_BITS * (q % 2)) & ((1 << BLOCK_BITS) - 1)
                    n = n.with_bounds(min_val=0, max_val=E * (REGION // P))
                    wait_apart(sp, rows_turned, s - XR + 1, ids_copied)
                    sp.dma_start(rows[:, q], sorted_rows[bass.ds(n * P, P)]).then_inc(rows_in[q], 16)

            run_tiles(sp, load_rows)

            for q in range(XR):
                sp.wait_ge(sent[q], 16 * (TILES // XR))
            by_chunk = results.rearrange("(k c i p) d -> c k p i d", k=2, p=P, i=CH)

            def load(c, half):
                wait_apart(sp, got_in[half], 16 * (c - half))
                for k in range(2):
                    sp.dma_start(got[k][:, bass.ts(c, CH)], by_chunk[c, k]).then_inc(got_in[half], 16)

            def store(c, half):
                wait_apart(sp, fin_done, c + 1)
                sp.dma_start(out_chunks[c], fin[:, half]).then_inc(out_sent[half], 16)

            run_chunks(sp, (0, load), (4, store))
            for half in range(2):
                sp.wait_ge(out_sent[half], 16 * (NCH // 2))

        @block.gpsimd
        def _(pool):
            pool.memset(ident[:, :], 0.0).then_inc(consts, 1)
            pool.memset(causal_neg[:, :], 0.0).then_inc(consts, 1)
            pool.memset(minus_half[:, :], -0.5).then_inc(consts, 1)
            pool.wait_ge(consts, 3)
            pool.affine_select(out=ident[:, :], in_=ident[:, :], compare_op=ALU.not_equal, fill=1.0, base=0,
                               pattern=[[-1, P]], channel_multiplier=1).then_inc(consts, 1)
            pool.affine_select(out=causal_neg[:, :], in_=causal_neg[:, :], compare_op=ALU.is_ge, fill=NEG, base=0,
                               pattern=[[-1, P]], channel_multiplier=1).then_inc(consts, 1)
            pool.wait_ge(consts, 5)
            pool.tensor_copy(ident_bf[:, :], ident[:, :]).then_inc(consts, 1)
            pool.memset(zeroed(k_stack[0:SHIFT, 0]), 0).then_inc(keys_zeroed[0], 1)

            def more_constants():
                pool.wait_ge(l_split, 1)
                pool.memset(zeroed(k_stack[SHIFT:P, :].rearrange("p r h q -> p (r h) q")), 0x3F803F80).then_inc(stack_ones, 1)
                pool.wait_ge(stack_ones, 1)
                for i in (1, 2):
                    pool.memset(zeroed(k_stack[0:SHIFT, i]), 0).then_inc(keys_zeroed[i], 1)
                    pool.wait_ge(keys_zeroed[i], 1)
                pool.memset(v_aug[:, :, :, :, HD:32], 0.0).then_inc(consts_p, 1)
                pool.wait_ge(consts_p, 1)
                pool.memset(v_aug[:, :, :, :, HD:HD + 1], 1.0).then_inc(consts_p, 1)
                pool.memset(earlier[:, :], 1.0).then_inc(iotas, 1)
                pool.memset(pad[:, :, :], 0.0).then_inc(iotas, 1)
                pool.iota(place[:, :, :, :].rearrange("p b i k -> p (b i) k"), pattern=[[P, NT], [N, 2]], base=0,
                          channel_multiplier=1).then_inc(iotas, 1)
                pool.iota(tile_no_i[:, :], pattern=[[0, 1]], base=0, channel_multiplier=1).then_inc(iotas, 1)
                pool.wait_ge(iotas, 4)
                pool.affine_select(out=earlier[:, :], in_=earlier[:, :], compare_op=ALU.is_gt, fill=0.0, base=0,
                                   pattern=[[1, P]], channel_multiplier=-1).then_inc(iotas, 1)
                pool.memset(pad[:, :, D:ROW].bitcast(U32), 2 * N).then_inc(iotas, 1)

            pool.wait_ge(weights_in, 96)

            def body(t, r, lap):
                for u in range(NP):
                    s, n = s_unit(t, u)
                    if on(s) and n % 2 == 0:
                        wait_apart(pool, exp_done, NP * s + n + 1)
                        for at, step in ((0, T), (2 * T, P)):
                            diag = probs[:, n, at:at + 2 * step].rearrange("p (h q) -> p h q", h=2)[:, :, 0:P]
                            last = pool.affine_select(out=diag, in_=diag, compare_op=ALU.is_ge, fill=0.0, base=0,
                                                      pattern=[[0, 2], [1, P]], channel_multiplier=-1)
                        last.then_inc(masked, 1)
                    if u == 0 and on(t - 4):
                        pool.wait_ge(var_done, t - 3)
                        pool.tensor_tensor(rstd[:, :], var_eps[:, :], minus_half[:, 0:TT], ALU.pow).then_inc(rstd_done, 1)
                        pool.wait_ge(rstd_done, t - 3)
                        pool.tensor_tensor(centre1[:, :], neg_mean[:, :], rstd[:, :], ALU.mult).then_inc(centred, 1)
                    if u == 2 and on(t - 4):
                        pool.wait_ge(yn_done, t - 3)
                        pool.tensor_tensor(yg[:, :, :], yn[:, :, :], gamma_all[:, None, :].broadcast_to([P, TT, D]),
                                           ALU.mult).then_inc(yg_done, 1)
                        pool.wait_ge(yg_done, t - 3)
                        pool.tensor_tensor(ys[:, :, :], yg[:, :, :], x_beta[:, :, :], ALU.add).then_inc(ys_done, 1)
                    if u == (0 if early(t) else 3) and on(t):
                        after(pool, stacked[r], 16 * 12 * lap)
                        pool.wait_ge(m_split, t + 1)
                        pool.tensor_tensor(part_l[:, r], rest[:, :, :], part_m[:, r], ALU.subtract).then_inc(l_split, 1)
                    if u == 3 and isinstance(t, int) and t == 0:
                        more_constants()
                    if u == 4 and on(t - 4):
                        pool.wait_ge(var2_done, t - 3)
                        pool.tensor_tensor(rstd2[:, :], var_eps2[:, :], minus_half[:, 0:TT], ALU.pow).then_inc(rstd2_done, 1)
                        pool.wait_ge(rstd2_done, t - 3)
                        pool.tensor_tensor(centre2[:, :], neg_mean2[:, :], rstd2[:, :], ALU.mult).then_inc(centred2, 1)
                    if u == 3 and on(t - 3):
                        pool.wait_ge(xres_in[r], 16 * lap)
                        after(pool, y_ready, t - 3)
                        xr = xres[:, (r - 3) % 3]
                        pool.tensor_tensor(x_bproj[:, :, :], xr, bproj_all[:, None, :].broadcast_to([P, TT, D]),
                                           ALU.add).then_inc(residuals, 1)
                        after(pool, ys_done, t - 3)
                        pool.tensor_tensor(x_beta[:, :, :], xr, beta_all[:, None, :].broadcast_to([P, TT, D]),
                                           ALU.add).then_inc(residuals, 1)
                    for n in {4: (0,), 5: (1,), 6: (2,), 7: (3,)}.get(u, ()) if on(t - 5) else ():
                        q = (r - 5) % 3
                        if n == 0:
                            wait_apart(pool, placed, t - 4, x2_twice, row_ready)
                            if isinstance(t, int) and t == B + 4:
                                pool.wait_ge(padded, 16 * (E + 1))
                        pool.indirect_dma_start(sorted_rows, bass.IndirectOffsetOnAxis(
                            ap=row_no[:, q * 2 * TT + n:q * 2 * TT + n + 1], axis=0), x2[:, q, n % 2, n // 2], None).then_inc(scattered[q], 16)

            run(pool, body)

            def send(s, q, turn):
                if is_tile(s - 3):
                    q = (q - 3) % XR
                    wait_apart(pool, y_biased, s - 2)
                    pool.indirect_dma_start(results, bass.IndirectOffsetOnAxis(ap=y_rows[:, q, D:ROW].bitcast(U32), axis=0),
                                            y_rows[:, q, 0:D], None, bounds_check=2 * N - 1, oob_is_err=False).then_inc(sent[q], 16)

            run_tiles(pool, send)

            def weigh(c, half):
                pool.wait_ge(got_in[half], 16 * (c - half) + 32)
                after(pool, moe_done, c - 1)
                pool.tensor_tensor(first[:, half], got[0][:, bass.ts(c, CH)],
                                   wgt[:, bass.ts(c, CH), 0:1].broadcast_to([P, CH, D]), ALU.mult).then_inc(first_done, 1)

            def add_up(c, half):
                pool.wait_ge(clipped_done, c + 1)
                residual = x2_all[:, bass.ts(c, 2), :].rearrange("p b (i d) -> p (b i) d", d=D)
                pool.tensor_tensor(residual, clipped[:, half], residual, ALU.add).then_inc(x3_done, 1)

            def invert(c, half):
                after(pool, fin_done, c - 1)
                pool.wait_ge(moe_var, c + 1)
                pool.tensor_tensor(rstd3[:, half], var_eps3[:, :], minus_half[:, :], ALU.pow).then_inc(moe_rstd, 1)

            run_chunks(pool, (0, weigh), (1, add_up), (2, invert))

        @block.scalar
        def _(act):
            act.wait_ge(consts, 6)
            act.activation(warm[:, :], minus_half[:, 0:1], ACT.Exp).then_inc(warmed, 1)

            def body(t, r, lap):
                for u in range(NP):
                    s, n = s_unit(t, u)
                    if on(s):
                        act.wait_ge(s_ready, NP * s + n + 1)
                        after(act, pv_done, 4 * s - 4 + n // 2 + 1)
                        act.activation(probs[:, n], S[n % 2][:, 0:3 * T], ACT.Exp, scale=SCALE).then_inc(exp_done, 1)
                    if u == (0 if early(t) else 1) and on(t):
                        act.wait_ge(xT_ready, t + 1)
                        act.copy(xT[:, r], G[:, 0:T]).then_inc(xT_copied, 1)
                    if u == 1 and on(t - 4):
                        act.wait_ge(centred, t - 3)
                        for i in range(TT):
                            last = act.activation(yn[:, i], y[:, i], ACT.Identity, bias=centre1[:, i:i + 1], scale=rstd[:, i:i + 1])
                        last.then_inc(yn_done, 1)
                    if u == (0 if early(t) else 2) and on(t):
                        act.wait_ge(qk_ready, t + 1)
                        after(act, stacked[r], 16 * 12 * lap)
                        act.copy(part_h[:, r], G[:, :].rearrange("p (w q) -> p w q", w=2)).then_inc(h_split, 1)
                    if u == (0 if early(t) else 3) and on(t):
                        act.wait_ge(rest_left, t + 1)
                        act.copy(part_m[:, r], rest[:, :, :]).then_inc(m_split, 1)
                    if u == 3 and on(t - 3):
                        act.wait_ge(pv_done, 4 * (t - 2))
                        after(act, o_turned, 2 * (t - 3))
                        act.copy(heads_t[:, 2:4], O[:, :].rearrange("p (k q) -> p k q", k=2)).then_inc(o_copied, 1)
                    if u == 4 and on(t):
                        act.wait_ge(v_ready, t + 1)
                        act.copy(v_aug[:, r, :, :, 0:HD],
                                 O[:, 0:T].rearrange("p (i h d) -> p i h d", i=TT, h=H)).then_inc(v_copied, 1)
                    if u == 5 and on(t - 4):
                        act.wait_ge(centred2, t - 3)
                        after(act, scattered[(r - 4) % 3], 16 * 2 * TT * (lap + (r - 4) // 3))
                        after(act, x2_kept, t - 4)
                        for i in range(TT):
                            last = act.activation(x2[:, (r - 4) % 3, 0, i, 0:D], ys[:, i], ACT.Identity, bias=centre2[:, i:i + 1],
                                                  scale=rstd2[:, i:i + 1])
                        last.then_inc(x2_done, 1)
                    if u == 3 and isinstance(t, int) and t == B + 3:
                        act.wait_ge(pad_rows_done, 1)
                        act.wait_ge(iotas, 6)
                        pad_experts(act, range(0, ACT_PADS))
                    if u == 6 and on(t - 4):
                        act.wait_ge(x2T_ready, t - 3)
                        act.copy(x2T[:, (r - 4) % 3], M[0][:, 0:T]).then_inc(x2T_copied, 1)
                    if u == 6 and on(t - 3):
                        act.wait_ge(on_turned, t - 2)
                        act.copy(heads_n_t[:, :], G[:, 0:T]).then_inc(on_copied, 1)
                    if u == 7 and on(t - 4):
                        act.wait_ge(x2_done, t - 3)
                        act.copy(x2[:, (r - 4) % 3, 1, :, 0:D], x2[:, (r - 4) % 3, 0, :, 0:D]).then_inc(x2_twice, 1)
                        act.copy(x2_all[:, t - 4].rearrange("p (i d) -> p i d", i=TT), x2[:, (r - 4) % 3, 0, :, 0:D]).then_inc(x2_kept, 1)
                    if u == 7 and isinstance(t, int) and t == B + 3:
                        pad_experts(act, range(ACT_PADS, 2 * ACT_PADS))
                    if u == 7 and on(t - 2):
                        act.wait_ge(pv_done, 4 * (t - 2) + 2)
                        after(act, o_turned, 2 * (t - 2))
                        act.copy(heads_t[:, 0:2], O[:, :].rearrange("p (k q) -> p k q", k=2)).then_inc(o_copied, 1)
                    if u == 7 and on(t - 1):
                        act.wait_ge(shift_turned, t)
                        after(act, shifted, 16 * (t - 3))
                        act.copy(shift_t[:, (r - 1) % 3], M1_bf[0:2 * H * TT, 0:P]).then_inc(shift_copied, 1)

            run(act, body)

            act.wait_ge(diff_done, 1)
            act.activation(exp2[:, :], diff[:, :], ACT.Exp).then_inc(exp2_done, 1)

            def layers(s, q, turn):
                if is_tile(s):
                    if q == XR - 1:
                        after(act, sent[q], 16 * turn)
                    act.wait_ge(rows_turned, s + 1)
                    after(act, h_ready, 2 * s - 2)
                    act.copy(rows_t[:, q % 2], (G, O)[q % 2][:, 0:P]).then_inc(rows_copied, 1)
                if is_tile(s - 1):
                    after(act, layer2_done, s - 2)
                    for f in range(FC):
                        act.wait_ge(h_ready, FC * (s - 1) + f + 1)
                        act.activation(hT[:, (q - 1) % 2, f], hidden[(q - 1) % 2 * FC + f], ACT.Gelu,
                                       bias=expert_now[:, (q - 1) % XR, AT_B1 + f:AT_B1 + f + 1]).then_inc(gelu_done, 1)

            run_tiles(act, layers)

            def weigh(c, half):
                act.wait_ge(got_in[half], 16 * (c - half) + 32)
                after(act, moe_done, c - 1)
                for i in range(CH):
                    last = act.activation(second[:, half, i], got[1][:, CH * c + i], ACT.Copy, scale=wgt[:, CH * c + i, 1:2])
                last.then_inc(second_done, 1)

            def finish(c, half):
                act.wait_ge(minus_mean_done, c + 1)
                after(act, out_sent[half], 8 * (c - half))
                for i in range(CH):
                    last = act.activation(fin[:, half, i], x3(c, i), ACT.Identity, bias=minus_mean[:, half, i:i + 1],
                                          scale=rstd3[:, half, i:i + 1])
                last.then_inc(fin_done, 1)

            run_chunks(act, (0, weigh), (3, finish))

        @block.vector
        def _(dve):
            dve.memset(zeroed(q_stack[:, 0]), 0).then_inc(queries_zeroed[0], 1)

            def more_constants():
                for i in (1, 2):
                    dve.memset(zeroed(q_stack[:, i]), 0).then_inc(queries_zeroed[i], 1)
                dve.memset(ones_bf[:, :], 1.0).then_inc(numbered, 1)
                dve.memset(ones_e[:, :], 1.0).then_inc(numbered, 1)
                dve.memset(seen[:, :], 0.0).then_inc(seen_done, 1)
                for e in range(E):
                    dve.memset(expert_no[:, e:e + 1], float(e)).then_inc(numbered, 1)
                    dve.memset(region_at[:, e:e + 1], float(e * REGION)).then_inc(numbered, 1)
                for q in range(XR):
                    dve.memset(expert_unit[:, q:q + 1], float(1 << EXPERT_BITS * q)).then_inc(numbered, 1)
                for q in range(2):
                    dve.memset(block_unit[:, q:q + 1], float(1 << BLOCK_BITS * q)).then_inc(numbered, 1)

            dve.wait_ge(weights_in, 96)
            dve.tensor_copy(wqk[:, :, :].rearrange("p w (d h) -> p w d h", d=HD),
                            wqk_raw[:, 0:2 * D].rearrange("p (w h d) -> p w d h", w=2, h=H)).then_inc(consts_v, 1)
            dve.wait_ge(gate_turned, 1)
            dve.tensor_copy(gate_t[:, :], M[0][:, 0:E]).then_inc(consts_v, 1)

            def split(t, r):
                dve.wait_ge(h_split, t + 1)
                after(dve, l_split, t)
                dve.tensor_tensor(rest[:, :, :], G[:, :].rearrange("p (w q) -> p w q", w=2), part_h[:, r],
                                  ALU.subtract).then_inc(rest_left, 1)
                if isinstance(t, int) and t == 0:
                    more_constants()

            def body(t, r, lap):
                if on(t) and early(t):
                    split(t, r)
                def reduce(i):
                    if not on(t - 1):
                        return
                    half, h0, nh = M_UNITS[i]
                    dve.wait_ge(m_ready, NM * (t - 1) + i + 1)
                    if i == 0:
                        after(dve, shift_made, t - 3)
                    dve.tensor_reduce(row_max[:, (r - 1) % 3, h0:h0 + nh, half],
                                      M[i % 2][:, :].rearrange("p (h k) -> p h k", h=nh), X, ALU.max).then_inc(m_reduced, 1)

                def turned_heads(i):
                    return G[:, :].rearrange("p (h c) -> p h c", h=H)

                def invert_sums(i):
                    dve.wait_ge(o_turned, 2 * (t - 3) + i + 1)
                    dve.reciprocal(inv_sum[:, i], turned_heads(i)[:, :, HD]).then_inc(inverted, 1)

                def normalise_heads(i):
                    dve.wait_ge(inverted, 2 * (t - 3) + i + 1)
                    after(dve, on_turned, t - 3)
                    dve.tensor_tensor(heads[:, i].rearrange("p (h d) -> p h d", h=H), turned_heads(i)[:, :, 0:HD],
                                      inv_sum[:, i, :, None].broadcast_to([P, H, HD]), ALU.mult).then_inc(o_normed, 1)

                reduce(0)
                if on(t - 4):
                    dve.wait_ge(y_ready, t - 3)
                    for i in range(TT):
                        dve.bn_stats(stats[:, i], y[:, i]).then_inc(stats_done, 1)
                if on(t - 5):
                    dve.wait_ge(top_kept, 2 * (t - 4))
                    for k in range(2):
                        dve.tensor_tensor(chosen[:, :, k], top_i_f[:, :, k, None].broadcast_to([P, TT, E]),
                                          expert_no[:, None, :].broadcast_to([P, TT, E]), ALU.is_equal).then_inc(chosen_done, 1)
                if on(t - 4):
                    wait_apart(dve, stats_done, (2 * TT) * (t - 4) + TT)
                    for i in range(TT):
                        dve.bn_aggr(moments[:, i], stats[:, i]).then_inc(stats_done, 1)
                if on(t - 5):
                    dve.wait_ge(chosen_done, 2 * (t - 4))
                    dve.tensor_tensor(both[:, :, :], chosen[:, :, 0], chosen[:, :, 1], ALU.add).then_inc(both_done, 1)
                if on(t - 4):
                    dve.wait_ge(stats_done, 2 * TT * (t - 3))
                    after(dve, centred, t - 4)
                    dve.tensor_scalar(neg_mean[:, :], moments[:, :, 0], -1.0, None, ALU.mult)
                    dve.tensor_scalar(var_eps[:, :], moments[:, :, 1], EPS, None, ALU.add).then_inc(var_done, 1)
                reduce(1)
                reduce(2)
                if on(t - 5):
                    dve.wait_ge(rank_ready, t - 4)
                    dve.tensor_tensor(row_of[:, :, :], O[:, 0:TT * E].rearrange("p (i e) -> p i e", i=TT),
                                      region_at[:, None, :].broadcast_to([P, TT, E]), ALU.add).then_inc(rank_read, 1)
                    dve.tensor_tensor(seen[:, :], seen[:, :], both[:, 0], ALU.add).then_inc(row_done, 1)
                if on(t - 5):
                    dve.wait_ge(rank_read, t - 4)
                    for i in range(TT):
                        dve.tensor_tensor(row_chosen[:, 2 * i:2 * i + 2], chosen[:, i],
                                          row_of[:, i, None, :].broadcast_to([P, 2, E]), ALU.mult).then_inc(row_done, 1)
                reduce(3)
                if on(t - 5):
                    dve.wait_ge(row_done, (TT + 2) * (t - 5) + TT + 1)
                    dve.tensor_reduce(row_f[:, :], row_chosen[:, :, :], X, ALU.add).then_inc(row_done, 1)
                    dve.tensor_tensor(seen[:, :], seen[:, :], both[:, 1], ALU.add).then_inc(seen_done, 1)
                reduce(4)
                if on(t - 5):
                    wait_apart(dve, row_done, (TT + 2) * (t - 4))
                    q = (r - 5) % 3
                    dve.tensor_copy(row_no[:, q * 2 * TT:(q + 1) * 2 * TT], row_f[:, :]).then_inc(row_ready, 1)
                if isinstance(t, int) and t == B + 3:
                    dve.wait_ge(counts_ready, 1)
                    dve.tensor_tensor(pad_row[:, :], G[:, 0:E], region_at[:, :], ALU.add).then_inc(pad_rows_done, 1)
                if on(t) and not early(t):
                    split(t, r)
                reduce(5)
                if on(t - 4):
                    dve.wait_ge(ys_done, t - 3)
                    for i in range(TT):
                        dve.bn_stats(stats2[:, i], ys[:, i]).then_inc(stats2_done, 1)
                reduce(6)
                if on(t - 4):
                    wait_apart(dve, stats2_done, (2 * TT) * (t - 4) + TT)
                    for i in range(TT):
                        dve.bn_aggr(moments2[:, i], stats2[:, i]).then_inc(stats2_done, 1)
                    dve.wait_ge(stats2_done, 2 * TT * (t - 3))
                    after(dve, centred2, t - 4)
                    dve.tensor_scalar(neg_mean2[:, :], moments2[:, :, 0], -1.0, None, ALU.mult)
                    dve.tensor_scalar(var_eps2[:, :], moments2[:, :, 1], EPS, None, ALU.add).then_inc(var2_done, 1)
                reduce(7)
                if on(t - 3):
                    invert_sums(0)
                reduce(8)
                if on(t - 3):
                    normalise_heads(0)
                reduce(9)
                if on(t - 3):
                    invert_sums(1)
                reduce(10)
                if on(t - 3):
                    normalise_heads(1)
                if on(t - 4):
                    after(dve, scattered[(r - 4) % 3], 16 * 2 * TT * (lap + (r - 4) // 3))
                    dve.tensor_copy(x2[:, (r - 4) % 3, :, :, D].bitcast(U32),
                                    place[:, t - 4].rearrange("p i k -> p k i")).then_inc(placed, 1)
                reduce(11)
                if on(t - 1):
                    dve.wait_ge(m_reduced, NM * t)
                    after(dve, shift_turned, t - 3)
                    b = (r - 1) % 3
                    dve.tensor_scalar(shift[:, b, 0], row_max[:, b], -1.0, None, ALU.mult).then_inc(shift_hi, 1)
                    dve.wait_ge(shift_hi, t)
                    dve.scalar_tensor_tensor(out=shift[:, b, 1], in0=row_max[:, b], scalar=-1.0, in1=shift[:, b, 0],
                                             op0=ALU.mult, op1=ALU.subtract).then_inc(shift_made, 1)
                if on(t - 4):
                    dve.wait_ge(gate_ready, t - 3)
                    dve.tensor_copy(logits[:, (r - 4) % 3], M[0][:, T:T + TT * E].rearrange("p (i e) -> p i e", i=TT)).then_inc(logits_done, 1)
                    wait_apart(dve, logits_done, t - 3)
                    for i in range(TT):
                        dve.max(top_v[:, i], logits[:, (r - 4) % 3, i]).then_inc(top_done, 1)
                    wait_apart(dve, top_done, TT * (t - 3))
                    for i in range(TT):
                        dve.max_index(top_i[:, i], top_v[:, i], logits[:, (r - 4) % 3, i]).then_inc(index_done, 1)
                    dve.tensor_copy(top_v_all[:, t - 4], top_v[:, :, 0:2]).then_inc(top_kept, 1)
                if on(t - 3):
                    dve.wait_ge(proj_ready, t - 2)
                    dve.wait_ge(residuals, 2 * (t - 3) + 1)
                    after(dve, yn_done, t - 3)
                    dve.tensor_tensor(y[:, :, :], G[:, 0:T].rearrange("p (i d) -> p i d", i=TT), x_bproj[:, :, :],
                                      ALU.add).then_inc(y_ready, 1)
                if on(t - 4):
                    dve.wait_ge(index_done, TT * (t - 3))
                    dve.tensor_copy(top_i_f[:, :, :], top_i[:, :, 0:2]).then_inc(top_kept, 1)

            run(dve, body)

            dve.wait_ge(iotas, 4)
            dve.tensor_copy(tile_no[:, :], tile_no_i[:, :]).then_inc(numbered, 1)
            dve.wait_ge(top_kept, 2 * B)
            tv = top_v_all[:, :, :, :].rearrange("p b i k -> p (b i) k")
            dve.tensor_tensor(diff[:, :], tv[:, :, 1], tv[:, :, 0], ALU.subtract).then_inc(diff_done, 1)

            dve.wait_ge(counts_ready, 2)
            dve.tensor_scalar(rounded[:, :], G[:, 0:E], float(P - 1), None, ALU.add).then_inc(table, 1)
            dve.wait_ge(table, 1)
            dve.tensor_scalar(tiles_i[:, :], rounded[:, :], P.bit_length() - 1, None, ALU.arith_shift_right).then_inc(table, 1)
            wait_apart(dve, table, 2)
            dve.tensor_copy(tiles[:, :], tiles_i[:, :]).then_inc(table, 1)
            dve.wait_ge(table, 3)
            dve.tensor_tensor_scan(tiles_end[:, :], ones_e[:, :], tiles[:, :], 0.0, ALU.mult, ALU.add).then_inc(table, 1)
            dve.tensor_scalar(skip[:, :], tiles[:, :], -1.0, float(REGION // P), ALU.mult, ALU.add).then_inc(table, 1)
            dve.wait_ge(table, 5)
            dve.wait_ge(numbered, 3 + 2 * E + XR + 2)
            dve.tensor_scalar(ended[:, :], tiles_end[:, :], tile_no[:, 0:1], None, ALU.is_le).then_inc(table, 1)
            dve.wait_ge(table, 6)
            dve.tensor_tensor(skipped[:, :], ended[:, :], skip[:, :], ALU.mult).then_inc(table, 1)
            dve.tensor_reduce(n_ended[:, :], ended[:, :], X, ALU.add).then_inc(table, 1)
            dve.wait_ge(table, 8)
            dve.tensor_reduce(n_skipped[:, :], skipped[:, :], X, ALU.add).then_inc(table, 1)
            dve.tensor_scalar(tile_f[:, 0:1], n_ended[:, :], float(E - 1), None, ALU.min).then_inc(tile_f_done, 1)
            dve.wait_ge(table, 9)
            dve.tensor_tensor(tile_f[:, 1:2], tile_no[:, :], n_skipped[:, :], ALU.add).then_inc(tile_f_done, 1)
            dve.wait_ge(tile_turned, 1)
            dve.tensor_tensor(expert_part[:, :].rearrange("p (i q) -> p i q", q=XR),
                              G[0:1, 0:TILES].rearrange("p (i q) -> p i q", q=XR),
                              expert_unit[:, None, :].broadcast_to([1, TILES // XR, XR]), ALU.mult).then_inc(tile_parts, 1)
            dve.scalar_tensor_tensor(out=block_part[:, :].rearrange("p (i q) -> p i q", q=2),
                                     in0=G[0:1, P:P + TILES].rearrange("p (i q) -> p i q", q=2), scalar=float(E * (REGION // P)),
                                     in1=block_unit[:, None, :].broadcast_to([1, TILES // 2, 2]),
                                     op0=ALU.min, op1=ALU.mult).then_inc(tile_parts, 1)
            dve.wait_ge(tile_parts, 2)
            dve.tensor_reduce(expert_sum[:, :], expert_part[:, :].rearrange("p (i q) -> p i q", q=XR), X, ALU.add).then_inc(tile_sums, 1)
            dve.tensor_reduce(block_sum[:, :], block_part[:, :].rearrange("p (i q) -> p i q", q=2), X, ALU.add).then_inc(tile_sums, 1)
            dve.wait_ge(tile_sums, 2)
            dve.tensor_copy(expert_word[:, :], expert_sum[:, :]).then_inc(words_done, 1)
            dve.tensor_copy(block_word[:, :], block_sum[:, :]).then_inc(words_done, 1)
            dve.wait_ge(exp2_done, 1)
            dve.tensor_scalar(esum[:, :], exp2[:, :], 1.0, None, ALU.add).then_inc(wt, 1)
            dve.wait_ge(wt, 1)
            dve.reciprocal(wgt[:, :, 0], esum[:, :]).then_inc(wt, 1)
            dve.wait_ge(wt, 2)
            dve.tensor_tensor(wgt[:, :, 1], wgt[:, :, 0], exp2[:, :], ALU.mult).then_inc(wt, 1)
            dve.wait_ge(words_done, 2)
            dve.wait_ge(experts_in, 96)
            dve.wait_ge(pv_done, 4 * B)
            word = [0]

            def layers(s, q, turn):
                if is_tile(s):
                    if q == 0:
                        word[0] = experts_of(dve, turn)
                    e = expert(word[0], q)
                    after(dve, y_biased, s - XR + 1)
                    dve.tensor_copy(expert_now[:, q], experts[:, bass.ds(e * SIZE, SIZE)]).then_inc(expert_ready, 1)
                if is_tile(s - 1):
                    slot = (q - 1) % XR
                    if q >= 1:
                        after(dve, sent[slot], 16 * turn)
                    else:
                        after(dve, rows_copied, s)
                    dve.wait_ge(rows_turned, s)
                    dve.tensor_copy(y_rows[:, slot, D:ROW].bitcast(U32), rows[:, slot, D:ROW].bitcast(U32)).then_inc(ids_copied, 1)
                if is_tile(s - 3):
                    slot = (q - 3) % XR
                    dve.wait_ge(layer2_done, s - 2)
                    dve.tensor_tensor(y_rows[:, slot, 0:D], M[(q - 3) % 2][:, 0:D], expert_now[:, slot, AT_B2:AT_W2],
                                      ALU.add).then_inc(y_biased, 1)

            run_tiles(dve, layers)

            def add_up(c, half):
                dve.wait_ge(first_done, c + 1)
                dve.wait_ge(second_done, c + 1)
                dve.tensor_tensor(moe[:, :, :], first[:, half], second[:, half], ALU.add).then_inc(moe_done, 1)
                dve.wait_ge(moe_done, c + 1)
                dve.tensor_tensor(acc[:, :, :], moe[:, :, :], x2_all[:, bass.ts(c, 2), :].rearrange("p b (i d) -> p (b i) d", d=D),
                                  ALU.add).then_inc(acc_done, 1)
                dve.wait_ge(acc_done, c + 1)
                after(dve, x3_done, c - 1)
                dve.tensor_scalar(clipped[:, half], acc[:, :, :], 100.0, -100.0, ALU.min, ALU.max).then_inc(clipped_done, 1)

            def measure(c, half):
                wait_apart(dve, x3_done, c + 1)
                for i in range(CH):
                    last = dve.bn_stats(stats3[:, i], x3(c, i))
                last.then_inc(stats3_done, 1)
                wait_apart(dve, stats3_done, c + 1)
                for i in range(CH):
                    last = dve.bn_aggr(moments3[:, i], stats3[:, i])
                last.then_inc(moe_aggr, 1)
                dve.wait_ge(moe_aggr, c + 1)
                dve.tensor_scalar(var_eps3[:, :], moments3[:, :, 1], EPS, None, ALU.add).then_inc(moe_var, 1)

            def centre(c, half):
                dve.wait_ge(moe_rstd, c + 1)
                after(dve, fin_done, c - 1)
                dve.scalar_tensor_tensor(out=minus_mean[:, half], in0=moments3[:, :, 0], scalar=-1.0, in1=rstd3[:, half],
                                         op0=ALU.mult, op1=ALU.mult).then_inc(minus_mean_done, 1)

            run_chunks(dve, (1, add_up), (3, centre), (2, measure))

        @block.tensor
        def _(pe):
            pe.wait_ge(consts, 6)
            pe.wait_ge(weights_in, 96)
            pe.transpose(M[0][:, 0:E], gate_raw[:, :], ident[0:E, 0:E]).then_inc(gate_turned, 1)
            pe.wait_ge(consts_v, 2)

            def scores(t, r, s, n):
                after(pe, exp_done, NP * s + n - 1)
                if n == 0:
                    pe.wait_ge(shifted, 16 * (s + 1))
                    if isinstance(t, int) and t == 2:
                        pe.wait_ge(numbered, 2 + 2 * E + XR + 2)
                        pe.wait_ge(stack_ones, 1)
                b = (r - (2 if n < NP - 2 else 3)) % 3
                for j in range(2):
                    h = 2 * n + j
                    pe.matmul(S[n % 2][:, j * T:j * T + T], k_stack[:, b, h, 0:P], q_stack[:, b, h, :],
                              start=(j == 0), stop=True, skip_group_check=True)
                for j in range(2):
                    h = 2 * n + j
                    last = pe.matmul(S[n % 2][:, 2 * T + j * P:2 * T + j * P + P], k_stack[:, b, h, P:T],
                                     q_stack[:, b, h, P:T], start=(j == 0), stop=True, skip_group_check=True)
                if n % 2:
                    for at, step in ((0, T), (2 * T, P)):
                        diag = S[n % 2][:, at:at + 2 * step].rearrange("p (h q) -> p h q", h=2)[:, :, 0:P]
                        last = pe.matmul(diag, causal_neg[:, :], ident_bf[:, None, :].broadcast_to([P, 2, P]), start=False,
                                         stop=True, skip_group_check=True)
                last.then_inc(s_ready, 1)

            def maxima(t, r, lap, i):
                half, h0, nh = M_UNITS[i]
                keys = P * (half + 1)
                if i == 0:
                    pe.wait_ge(stacked[(r - 1) % 3], 16 * 12 * (lap + (r - 1) // 3 + 1))
                    if on(t - 5):
                        pe.wait_ge(logits_done, t - 4)
                if i == 1 and on(t - 2):
                    pe.wait_ge(shift_copied, t - 1)
                after(pe, m_reduced, NM * (t - 1) + i - 1)
                b = (r - 1) % 3
                bank = M[i % 2]
                for j in range(nh):
                    pe.matmul(bank[:, j * keys:j * keys + keys], q_stack[0:SHIFT, b, h0 + j, half * P:half * P + P],
                              k_stack[0:SHIFT, b, h0 + j, 0:keys], start=(j == 0), stop=False, skip_group_check=True)
                diag = bank[:, :].rearrange("p (h k) -> p h k", h=nh)[:, :, keys - P:keys]
                pe.matmul(diag, ident_bf[:, :], causal_neg[:, None, :].broadcast_to([P, nh, P]), start=False, stop=True,
                          skip_group_check=True).then_inc(m_ready, 1)

            def values(t, r, s, k):
                pe.wait_ge(masked, NP // 2 * s + k + 1)
                pe.wait_ge(exp_done, NP * s + 2 * k + 2)
                if k == 0:
                    pe.wait_ge(v_copied, s + 1)
                    if isinstance(t, int) and t == 2:
                        pe.wait_ge(consts_p, 2)
                if k % 2 == 0:
                    after(pe, o_copied, 2 * s + k // 2)
                b = (r - (2 if k < 2 else 3)) % 3
                at = (k % 2) * T
                for j in range(4):
                    h = 4 * k + j
                    pe.matmul(O[32 * j:32 * j + 32, at:at + T], v_aug[:, b, 0, h], probs[:, h // 2, (h % 2) * T:(h % 2) * T + T],
                              start=True, stop=False, skip_group_check=True)
                for j in range(4):
                    h = 4 * k + j
                    last = pe.matmul(O[32 * j:32 * j + 32, at + P:at + T], v_aug[:, b, 1, h],
                                     probs[:, h // 2, 2 * T + (h % 2) * P:2 * T + (h % 2) * P + P],
                                     start=False, stop=True, skip_group_check=True)
                last.then_inc(pv_done, 1)

            def turn_heads(t, i):
                for k in range(4):
                    last = pe.transpose(G[:, k * P:k * P + P], heads_t[:, k, i * P:i * P + P], ident[:, :])
                last.then_inc(o_turned, 1)

            def turn_x(t, r, lap):
                if on(t - 4):
                    pe.wait_ge(y_ready, t - 3)
                elif on(t - 1):
                    pe.wait_ge(rest_left, t)
                pe.wait_ge(x_in[r], 16 * (lap + 1))
                for i in range(TT):
                    last = pe.transpose(G[:, i * P:i * P + P], xin[:, r, i], ident[:, :])
                last.then_inc(xT_ready, 1)

            def project(t, r):
                pe.wait_ge(xT_copied, t + 1)
                for w in range(2):
                    last = pe.matmul(G[:, w * T:w * T + T], wqk[:, w], xT[:, r], start=True, stop=True)
                last.then_inc(qk_ready, 1)

            def body(t, r, lap):
                for u in range(NP):
                    s, n = s_unit(t, u)
                    if on(s):
                        scores(t, r, s, n)
                    if u == 7 and on(t - 4):
                        pe.wait_ge(x2T_copied, t - 3)
                        for i in range(TT):
                            last = pe.matmul(M[0][:, T + i * E:T + i * E + E], x2T[:, (r - 4) % 3, i * P:i * P + P], gate_t[:, :],
                                             start=True, stop=True)
                        last.then_inc(gate_ready, 1)
                    if u == 0 and on(t) and early(t):
                        turn_x(t, r, lap)
                        project(t, r)
                    if on(t - 1):
                        for i in m_units(u):
                            maxima(t, r, lap, i)
                    if u == 1 and on(t) and not early(t):
                        turn_x(t, r, lap)
                    if u == 1 and on(t - 5):
                        pe.wait_ge(both_done, t - 4)
                        pe.wait_ge(seen_done, t - 4)
                        if on(t - 3):
                            pe.wait_ge(o_copied, 2 * (t - 3) + 1)
                        for i in range(TT):
                            rank = O[:, i * E:i * E + E]
                            pe.matmul(rank, earlier[:, :], both[:, i], start=True, stop=False, skip_group_check=True)
                            for j in range(i):
                                pe.matmul(rank, ones_bf[:, :], both[:, j], start=False, stop=False, skip_group_check=True)
                            last = pe.matmul(rank, ones_bf[:, :], seen[:, :], start=False, stop=True, skip_group_check=True)
                        last.then_inc(rank_ready, 1)
                    if u == 2 and isinstance(t, int) and t == B + 3:
                        pe.wait_ge(seen_done, B)
                        pe.wait_ge(y_ready, B)
                        pe.matmul(G[:, 0:E], ones_bf[:, :], seen[:, :], start=True, stop=True).then_inc(counts_ready, 1)
                    if u == 2 and on(t) and not early(t):
                        project(t, r)
                    if u == 4 and on(t - 3):
                        pe.wait_ge(o_copied, 2 * (t - 2))
                        if on(t):
                            pe.wait_ge(rest_left, t + 1)
                        elif on(t - 4):
                            pe.wait_ge(y_ready, t - 3)
                        turn_heads(t, 0)
                    if u == 4 and on(t):
                        if on(t - 3):
                            pe.wait_ge(o_copied, 2 * (t - 2))
                        if on(t - 1):
                            pe.wait_ge(v_copied, t)
                        pe.wait_ge(xT_copied, t + 1)
                        for i in range(TT):
                            last = pe.matmul(O[:, i * P:i * P + P], xT[:, r, i * P:i * P + P], wqk_raw[:, 2 * D:3 * D],
                                             start=True, stop=True)
                        last.then_inc(v_ready, 1)
                    if u == 5 and on(t - 3):
                        pe.wait_ge(o_normed, 2 * (t - 3) + 1)
                        turn_heads(t, 1)
                    if pv_quad(t, u) and on(pv_quad(t, u)[0]):
                        if u == 2 and on(t - 5):
                            pe.wait_ge(rank_read, t - 4)
                        if u == 5 and on(t):
                            pe.wait_ge(v_copied, t + 1)
                        values(t, r, *pv_quad(t, u))
                    if u == 6 and on(t - 4):
                        pe.wait_ge(x2_done, t - 3)
                        if on(t - 1):
                            pe.wait_ge(m_reduced, NM * t - 1)
                        after(pe, logits_done, t - 4)
                        for i in range(TT):
                            last = pe.transpose(M[0][:, i * P:i * P + P], x2[:, (r - 4) % 3, 0, i, 0:D], ident[:, :])
                        last.then_inc(x2T_ready, 1)
                    if u == 6 and on(t - 3):
                        pe.wait_ge(o_normed, 2 * (t - 2))
                        for i in range(TT):
                            last = pe.transpose(G[:, i * P:i * P + P], heads[:, i], ident[:, :])
                        last.then_inc(on_turned, 1)
                    if u == 7 and on(t - 1):
                        wait_apart(pe, shift_made, t)
                        pe.transpose(M1_bf[0:2 * H * TT, 0:P], shift[:, (r - 1) % 3].rearrange("p w h i -> p (w h i)"),
                                     ident_bf[:, :]).then_inc(shift_turned, 1)
                    if u == 7 and on(t - 3):
                        pe.wait_ge(on_copied, t - 2)
                        for i in range(TT):
                            last = pe.matmul(G[:, i * P:i * P + P], heads_n_t[:, i * P:i * P + P], wproj[:, :],
                                             start=True, stop=True)
                        last.then_inc(proj_ready, 1)

            run(pe, body)

            pe.wait_ge(seen_done, B + 1)
            pe.wait_ge(pad_rows_done, 1)
            pe.matmul(G[:, 0:E], ones_bf[:, :], seen[:, :], start=True, stop=True).then_inc(counts_ready, 1)
            pe.wait_ge(tile_f_done, 2)
            for w in range(2):
                last = pe.transpose(G[0:1, w * P:w * P + P], tile_f[:, w:w + 1], ident[:, :])
            last.then_inc(tile_turned, 1)
            pe.wait_ge(words_done, 2)
            pe.wait_ge(experts_in, 96)
            pe.wait_ge(o_copied, 2 * B)
            pe.wait_ge(exp_done, NP * B)
            pe.wait_ge(m_reduced, NM * B)

            def layers(s, q, turn):
                if is_tile(s):
                    pe.wait_ge(rows_in[q], 16 * (turn + 1))
                    after(pe, rows_copied, s - 1)
                    pe.transpose((G, O)[q % 2][:, 0:P], rows[:, q, 0:D], ident[:, :]).then_inc(rows_turned, 1)
                if is_tile(s - 1):
                    pe.wait_ge(rows_copied, s)
                    pe.wait_ge(expert_ready, s)
                    after(pe, gelu_done, FC * (s - 2))
                    for f in range(FC):
                        pe.matmul(hidden[(q - 1) % 2 * FC + f], expert_now[:, (q - 1) % XR, f * P:f * P + P], rows_t[:, (q - 1) % 2],
                                  start=True, stop=True).then_inc(h_ready, 1)
                if is_tile(s - 2):
                    pe.wait_ge(gelu_done, FC * (s - 1))
                    after(pe, y_biased, s - 3)
                    for f in range(FC):
                        last = pe.matmul(M[q % 2][:, 0:D], hT[:, q % 2, f], expert_now[:, (q - 2) % XR, AT_W2 + f * D:AT_W2 + f * D + D],
                                         start=(f == 0), stop=(f == FC - 1))
                    last.then_inc(layer2_done, 1)

            run_tiles(pe, layers)


_INS = ['L0_attn_target', 'L0_attn_w_qkv', 'L0_attn_w_proj', 'L0_attn_b_proj', 'L0_attn_ln_gamma', 'L0_attn_ln_beta',
        'L0_ffn_gate_w', 'L0_ffn_w1', 'L0_ffn_b1', 'L0_ffn_w2', 'L0_ffn_b2']
_OUTS = [((16, 256, 128), 'float32')]


def kernel(**inputs):
    import numpy as _np
    import concourse.bacc as _bacc
    from concourse import mybir as _mybir
    from concourse.bass_utils import run_bass_kernel_spmd as _run

    nc = _bacc.Bacc("TRN2", target_bir_lowering=False, num_devices=1)
    arrays, args = {}, []
    for name in _INS:
        a = _np.ascontiguousarray(inputs[name])
        arrays[f"in_{name}_dram"] = a
        args.append(nc.dram_tensor(f"in_{name}_dram", a.shape, _mybir.dt.from_np(a.dtype), kind="ExternalInput").ap())
    for i, (shape, dtype) in enumerate(_OUTS):
        dt = _mybir.dt.from_np(_np.dtype(dtype))
        args.append(nc.dram_tensor(f"out_{i}_dram", shape, dt, kind="ExternalOutput").ap())
    transformer_layer(nc, *args)
    r = _run(nc, [arrays], core_ids=[0])
    got = tuple(r.results[0][f"out_{i}_dram"] for i in range(len(_OUTS)))
    return got[0]
```
